# Optimizing a Trainium2 kernel written in Bass

```python
import numpy as np
import jax
import jax.numpy as jnp

def _softmax(x, axis=-1):
    return jax.nn.softmax(x, axis=axis)

def _gelu(x):
    return jax.nn.gelu(x, approximate=True)

def _silu(x):
    return jax.nn.silu(x)

def _sigmoid(x):
    return jax.nn.sigmoid(x)

def _layernorm(x, axis=-1, eps=1e-05):
    m = jnp.mean(x, axis=axis, keepdims=True)
    v = jnp.var(x, axis=axis, keepdims=True)
    return (x - m) / jnp.sqrt(v + eps)

def _scatter_add(tgt, idx, src, axis=0):
    return tgt.at[idx].add(src)

def _segment_sum(src, seg, n):
    return jax.ops.segment_sum(src, seg, n)
kernel_name = 'mk_decoder_preln_d1_seqx_r4_3df671'

def setup_inputs(seed: int=0):
    np.random.seed(seed)
    _w = jnp.asarray

    def _rec_inputs():
        import jax
        import jax.numpy as jnp
        _rk = jax.random.key(seed)
        x = -0.0002928 + 1 * jax.random.normal(jax.random.fold_in(_rk, 1), (64, 256, 256), jnp.float32)
        _lenS = 256 - jax.random.randint(jax.random.fold_in(_rk, 7), (64,), 0, max(1, 256 // 4) + 1, jnp.int32)
        _lenS2 = 120 - jax.random.randint(jax.random.fold_in(_rk, 8), (64,), 0, max(1, 120 // 4) + 1, jnp.int32)
        _ctx_1024P = jax.random.normal(jax.random.fold_in(_rk, 11), (64, 16, 256), jnp.float32)
        _ctx_1024c = jax.random.dirichlet(jax.random.fold_in(_rk, 511), 0.3 * jnp.ones((16,), jnp.float32), (64, 120))
        _ctx_1024t = jnp.einsum('bsk,bkd->bsd', _ctx_1024c, _ctx_1024P)
        _ctx_1024t = _ctx_1024t * jax.lax.rsqrt(jnp.mean(jnp.square(_ctx_1024t)) + 1e-12) * 0.953939
        ctx_1024 = -1.39393e-06 + 0.999914 * (_ctx_1024t + 0.3 * jax.random.normal(jax.random.fold_in(_rk, 611), (64, 120, 256), jnp.float32))
        return (x, ctx_1024)
    x, ctx_1024 = _rec_inputs()

    def _L0_attn_setup():
        import jax, jax.numpy as jnp
        import numpy as np
        DIM = 256
        NUM_HEADS = 16
        HEAD_DIM = DIM // NUM_HEADS
        B, L = (4, 512)

        def _alibi_bias_causal(seq_len, dtype):
            h = jnp.arange(1, NUM_HEADS + 1, dtype=jnp.float32)
            slopes = jnp.power(2.0, -8.0 * h / NUM_HEADS)
            pos = jnp.arange(seq_len, dtype=jnp.float32)
            rel = jnp.abs(pos[:, None] - pos[None, :])
            bias = -slopes[:, None, None] * rel[None, :, :]
            causal = pos[:, None] >= pos[None, :]
            bias = jnp.where(causal[None, :, :], bias, -jnp.inf)
            return bias.astype(dtype)
        key = jax.random.key(seed)
        ks = jax.random.split(key, 9)
        s = 0.02
        return {'x': jax.random.normal(ks[0], (B, L, DIM), jnp.float32), 'Wq': jax.random.normal(ks[1], (DIM, DIM), jnp.float32) * s, 'bq': jax.random.normal(ks[2], (DIM,), jnp.float32) * s, 'Wk': jax.random.normal(ks[3], (DIM, DIM), jnp.float32) * s, 'bk': jax.random.normal(ks[4], (DIM,), jnp.float32) * s, 'Wv': jax.random.normal(ks[5], (DIM, DIM), jnp.float32) * s, 'bv': jax.random.normal(ks[6], (DIM,), jnp.float32) * s, 'Wo': jax.random.normal(ks[7], (DIM, DIM), jnp.float32) * s, 'bo': jax.random.normal(ks[8], (DIM,), jnp.float32) * s}
    _L0_attn_all = _L0_attn_setup()
    _L0_attn_in = {k: v for k, v in _L0_attn_all.items() if k in ('Wq', 'bq', 'Wk', 'bk', 'Wv', 'bv', 'Wo', 'bo')}
    del _L0_attn_all

    def _L0_xattn_setup():
        import jax, jax.numpy as jnp
        import numpy as np
        DIM = 256
        NUM_HEADS = 16
        HEAD_DIM = DIM // NUM_HEADS
        key = jax.random.key(seed)
        ks = jax.random.split(key, 11)
        B, N, C = (2, 512, DIM)
        s = 1.0 / np.sqrt(C)
        inp = {'q': jax.random.normal(ks[0], (B, N, C), jnp.float32), 'k': jax.random.normal(ks[1], (B, N, C), jnp.float32), 'v': jax.random.normal(ks[2], (B, N, C), jnp.float32), 'Wq': jax.random.normal(ks[3], (C, C), jnp.float32) * s, 'bq': jnp.zeros((C,), jnp.float32), 'Wk': jax.random.normal(ks[4], (C, C), jnp.float32) * s, 'bk': jnp.zeros((C,), jnp.float32), 'Wv': jax.random.normal(ks[5], (C, C), jnp.float32) * s, 'bv': jnp.zeros((C,), jnp.float32), 'Wo': jax.random.normal(ks[6], (C, C), jnp.float32) * s, 'bo': jnp.zeros((C,), jnp.float32)}
        return inp
    _L0_xattn_all = _L0_xattn_setup()
    _L0_xattn_in = {k: v for k, v in _L0_xattn_all.items() if k in ('Wq', 'bq', 'Wk', 'bk', 'Wv', 'bv', 'Wo', 'bo')}
    del _L0_xattn_all

    def _L0_ffn_setup():
        import jax, jax.numpy as jnp
        import numpy as np
        D_MODEL = 256
        key = jax.random.key(seed)
        k_x, k_w, k_a1, k_a2 = jax.random.split(key, 4)
        x = jax.random.normal(k_x, (4, 512, D_MODEL), dtype=jnp.float32)
        weight = jax.random.normal(k_w, (D_MODEL, D_MODEL), dtype=jnp.float32) * 0.02
        aux_weight1 = jax.random.normal(k_a1, (D_MODEL, D_MODEL), dtype=jnp.float32) * 0.02
        aux_weight2 = jax.random.normal(k_a2, (D_MODEL, D_MODEL), dtype=jnp.float32) * 0.02
        bias = jnp.zeros((D_MODEL,), dtype=jnp.float32)
        return {'x': x, 'weight': weight, 'aux_weight1': aux_weight1, 'aux_weight2': aux_weight2, 'bias': bias}
    _L0_ffn_all = _L0_ffn_setup()
    _L0_ffn_in = {k: v for k, v in _L0_ffn_all.items() if k in ('weight', 'aux_weight1', 'aux_weight2', 'bias')}
    del _L0_ffn_all
    return {'x': x, 'ctx_1024': ctx_1024, 'L0_attn_Wq': _L0_attn_in['Wq'], 'L0_attn_bq': _L0_attn_in['bq'], 'L0_attn_Wk': _L0_attn_in['Wk'], 'L0_attn_bk': _L0_attn_in['bk'], 'L0_attn_Wv': _L0_attn_in['Wv'], 'L0_attn_bv': _L0_attn_in['bv'], 'L0_attn_Wo': _L0_attn_in['Wo'], 'L0_attn_bo': _L0_attn_in['bo'], 'L0_xattn_Wq': _L0_xattn_in['Wq'], 'L0_xattn_bq': _L0_xattn_in['bq'], 'L0_xattn_Wk': _L0_xattn_in['Wk'], 'L0_xattn_bk': _L0_xattn_in['bk'], 'L0_xattn_Wv': _L0_xattn_in['Wv'], 'L0_xattn_bv': _L0_xattn_in['bv'], 'L0_xattn_Wo': _L0_xattn_in['Wo'], 'L0_xattn_bo': _L0_xattn_in['bo'], 'L0_ffn_weight': _L0_ffn_in['weight'], 'L0_ffn_aux_weight1': _L0_ffn_in['aux_weight1'], 'L0_ffn_aux_weight2': _L0_ffn_in['aux_weight2'], 'L0_ffn_bias': _L0_ffn_in['bias']}

def reference(x, ctx_1024, L0_attn_Wq, L0_attn_bq, L0_attn_Wk, L0_attn_bk, L0_attn_Wv, L0_attn_bv, L0_attn_Wo, L0_attn_bo, L0_xattn_Wq, L0_xattn_bq, L0_xattn_Wk, L0_xattn_bk, L0_xattn_Wv, L0_xattn_bv, L0_xattn_Wo, L0_xattn_bo, L0_ffn_weight, L0_ffn_aux_weight1, L0_ffn_aux_weight2, L0_ffn_bias):
    import jax
    import jax.numpy as jnp

    def _L0_attn_ref(x, Wq, bq, Wk, bk, Wv, bv, Wo, bo):
        import jax, jax.numpy as jnp
        import numpy as np
        DIM = 256
        NUM_HEADS = 16
        HEAD_DIM = DIM // NUM_HEADS
        B, L = (4, 512)

        def _alibi_bias_causal(seq_len, dtype):
            h = jnp.arange(1, NUM_HEADS + 1, dtype=jnp.float32)
            slopes = jnp.power(2.0, -8.0 * h / NUM_HEADS)
            pos = jnp.arange(seq_len, dtype=jnp.float32)
            rel = jnp.abs(pos[:, None] - pos[None, :])
            bias = -slopes[:, None, None] * rel[None, :, :]
            causal = pos[:, None] >= pos[None, :]
            bias = jnp.where(causal[None, :, :], bias, -jnp.inf)
            return bias.astype(dtype)
        b, l, d = x.shape
        q = (jnp.einsum('bld,ed->ble', x, Wq) + bq).reshape(b, l, NUM_HEADS, HEAD_DIM).transpose(0, 2, 1, 3)
        k = (jnp.einsum('bld,ed->ble', x, Wk) + bk).reshape(b, l, NUM_HEADS, HEAD_DIM).transpose(0, 2, 1, 3)
        v = (jnp.einsum('bld,ed->ble', x, Wv) + bv).reshape(b, l, NUM_HEADS, HEAD_DIM).transpose(0, 2, 1, 3)
        scale = 1.0 / np.sqrt(HEAD_DIM)
        scores = jnp.einsum('bhqd,bhkd->bhqk', q, k) * scale
        scores = scores + _alibi_bias_causal(l, scores.dtype)[None]
        attn = jax.nn.softmax(scores, axis=-1)
        out = jnp.einsum('bhqk,bhkd->bhqd', attn, v)
        out = out.transpose(0, 2, 1, 3).reshape(b, l, d)
        return jnp.einsum('bld,ed->ble', out, Wo) + bo

    def _L0_xattn_ref(q, k, v, Wq, bq, Wk, bk, Wv, bv, Wo, bo):
        import jax, jax.numpy as jnp
        import numpy as np
        DIM = 256
        NUM_HEADS = 16
        HEAD_DIM = DIM // NUM_HEADS
        B, Nq, C = q.shape
        Nkv = k.shape[1]
        H, D = (NUM_HEADS, HEAD_DIM)
        qh = (q @ Wq.T + bq).reshape(B, Nq, H, D).transpose(0, 2, 1, 3)
        kh = (k @ Wk.T + bk).reshape(B, Nkv, H, D).transpose(0, 2, 1, 3)
        vh = (v @ Wv.T + bv).reshape(B, Nkv, H, D).transpose(0, 2, 1, 3)
        scale = D ** (-0.5)
        attn = jax.nn.softmax(jnp.einsum('bhqd,bhkd->bhqk', qh, kh) * scale, axis=-1)
        out = jnp.einsum('bhqk,bhkd->bhqd', attn, vh)
        out = out.transpose(0, 2, 1, 3).reshape(B, Nq, C)
        return out @ Wo.T + bo

    def _L0_ffn_ref(x, weight, aux_weight1, aux_weight2, bias):
        import jax, jax.numpy as jnp
        import numpy as np
        D_MODEL = 256
        h = jnp.einsum('btc,cd->btd', x, weight)
        h = jnp.einsum('btc,cd->btd', h, aux_weight1)
        h = jnp.einsum('btc,cd->btd', h, aux_weight2)
        return jnp.tanh(h + bias)
    x = x + _L0_attn_ref(_layernorm(x, axis=-1), L0_attn_Wq, L0_attn_bq, L0_attn_Wk, L0_attn_bk, L0_attn_Wv, L0_attn_bv, L0_attn_Wo, L0_attn_bo)
    x = x + _L0_xattn_ref(_layernorm(x, axis=-1), ctx_1024, ctx_1024, L0_xattn_Wq, L0_xattn_bq, L0_xattn_Wk, L0_xattn_bk, L0_xattn_Wv, L0_xattn_bv, L0_xattn_Wo, L0_xattn_bo)
    x = x + _L0_ffn_ref(_layernorm(x, axis=-1), L0_ffn_weight, L0_ffn_aux_weight1, L0_ffn_aux_weight2, L0_ffn_bias)
    return x

_drawn_inputs = setup_inputs


def setup_inputs(seed=0):
    import zlib

    import numpy as np

    out = dict(_drawn_inputs(seed))
    spreads = {'L0_xattn_bq': (0.0, 0.378),
     'L0_xattn_bk': (0.0, 2.0),
     'L0_xattn_bv': (0.0, 0.1),
     'L0_xattn_bo': (0.0, 0.1),
     'L0_ffn_bias': (0.0, 0.1)}
    factors = {'L0_attn_Wq': 8.0,
     'L0_attn_bq': 45.381,
     'L0_attn_Wk': 8.0,
     'L0_attn_bk': 64.0,
     'L0_attn_bv': 8.0,
     'L0_attn_bo': 3.322}
    for name, (base, spread) in spreads.items():
        noise = np.random.default_rng([zlib.crc32(name.encode()), seed]).standard_normal(out[name].shape)
        drawn = base * np.exp(spread * noise) if base else spread * noise
        out[name] = jnp.asarray(drawn.astype(out[name].dtype))
    for name, factor in factors.items():
        out[name] = (out[name] * factor).astype(out[name].dtype)
    return out
```

```python
from contextlib import ExitStack

import numpy as np

import concourse.bass as bass
from concourse import mybir

F32 = mybir.dt.float32
F32R = mybir.dt.float32r
BF16 = mybir.dt.bfloat16
ALU = mybir.AluOpType
ACT = mybir.ActivationFunctionType
AX = mybir.AxisListType

P = 128
NSEQ = 64
T = 256
D = 256
H = 16
HD = D // H
C = 120
NB = D // P
VW = HD + 1
AUG = 64
SHIFT = 96
EPS = 1e-5
BIG = -1e30
LAST = NSEQ - 1



def step_order(t):
    s, a, c, n = t, t - 1, t - 2, t + 1
    order = []

    def add(kind, b, part=0):
        if 0 <= b < NSEQ:
            order.append((kind, b, part))

    add("MAX", s, 0)
    add("HEADS_OUT", a, 0)
    add("HEADS_OUT", a, 1)
    add("XSCORE", c, 0)
    add("MAX", s, 1)
    if t % 2 == 0:
        add("LOAD_CTX", s)
    add("XSCORE", c, 1)
    add("OUT_T", a)
    add("MAX", s, 2)
    add("XSCORE", c, 2)
    add("OUT_PROJ", a)
    add("LOAD_X", n)
    add("MAX", s, 3)
    add("XSCORE", c, 3)
    add("XATTEND", c, 0)
    add("LN2", a)
    add("MAX", s, 4)
    add("XSCORE", c, 4)
    add("MAX", s, 5)
    add("XATTEND", c, 1)
    add("XSCORE", c, 5)
    add("MAX", s, 6)
    add("LN2_T", a)
    add("MAX", s, 7)
    add("XSCORE", c, 6)
    add("MAX", s, 8)
    add("XQ", a)
    add("XATTEND", c, 2)
    add("MAX", s, 9)
    add("XSCORE", c, 7)
    add("XQ_SAVE", a)
    add("MAX", s, 10)
    add("MAX", s, 11)
    add("MAX_T", s)
    add("MAX_STACK", s)
    add("XATTEND", c, 3)
    add("XQ_STACK", a)
    add("LN1", n)
    add("XHEADS_OUT", c, 0)
    add("XHEADS_OUT", c, 1)
    add("LN1_T", n)
    add("XOUT_T", c)
    add("Q", n)
    add("Q_SAVE", n)
    add("XOUT_PROJ", c)
    add("K", n)
    add("K_SAVE", n)
    add("LN3", c)
    add("SCORE", s, 0)
    add("SCORE", s, 1)
    add("V", n)
    add("SCORE", s, 2)
    add("Q_STACK", n)
    add("XMAX", a, 0)
    add("SCORE", s, 3)
    add("K_STACK", n)
    add("LN3_T", c)
    add("XMAX", a, 1)
    add("SCORE", s, 4)
    add("SCORE", s, 5)
    add("ATTEND", s, 0)
    add("XMAX", a, 2)
    add("SCORE", s, 6)
    add("FFN", c)
    add("SCORE", s, 7)
    add("XMAX", a, 3)
    add("SCORE", s, 8)
    if t % 2 == 0:
        add("CTX_T", s)
    add("SCORE", s, 9)
    add("ATTEND", s, 1)
    add("XMAX", a, 4)
    add("SCORE", s, 10)
    add("SCORE", s, 11)
    if t % 2 == 0:
        add("XK", s)
        add("XK_SAVE", s)
    add("XMAX", a, 5)
    add("SCORE", s, 12)
    add("SCORE", s, 13)
    add("ATTEND", s, 2)
    add("XMAX", a, 6)
    add("STORE", c)
    add("SCORE", s, 14)
    add("XV", s)
    add("SCORE", s, 15)
    add("XMAX", a, 7)
    add("XMAX_T", a)
    add("XMAX_STACK", a)
    add("XK_STACK", s)
    add("ATTEND", s, 3)
    return order


RINGS = {"max": 2, "score": 3, "attend": 1, "misc": 2}
FILLS = {
    "MAX": ("max", 12), "XMAX": ("max", 8),
    "SCORE": ("score", 16), "XSCORE": ("score", 8),
    "ATTEND": ("attend", 2), "XATTEND": ("attend", 2),
}
for _k in ("HEADS_OUT", "XHEADS_OUT"):
    FILLS[_k] = ("misc", 2)
for _k in ("LN1_T", "Q", "K", "V", "MAX_T", "OUT_T", "OUT_PROJ", "LN2_T", "XQ", "XMAX_T",
           "XOUT_T", "XOUT_PROJ", "LN3_T", "FFN", "CTX_T", "XK", "XV"):
    FILLS[_k] = ("misc", 1)
FIRST_STEP, LOOP_FROM, LOOP_TO, END_STEP = -1, 4, 62, NSEQ + 2


def bank_turns():
    held = {r: [None] * n for r, n in RINGS.items()}
    at = dict.fromkeys(RINGS, 0)
    turns = {}
    for t in range(FIRST_STEP, END_STEP):
        for kind, b, part in step_order(t):
            if kind not in FILLS:
                continue
            if kind in ("ATTEND", "XATTEND"):
                if part % 2:
                    continue
                part //= 2
            ring = FILLS[kind][0]
            bank = at[ring] % RINGS[ring]
            turns[kind, b, part] = bank, held[ring][bank]
            held[ring][bank] = kind, b, part
            at[ring] += 1
    for t in range(LOOP_FROM, LOOP_TO - 2):
        now = [k for k in step_order(t) if k in turns]
        for kind, b, part in now:
            bank, before = turns[kind, b, part]
            later, then = turns[kind, b + 2, part]
            assert bank == later and then == (before[0], before[1] + 2, before[2])
    return turns


def build(nc, x, ctx, wts, bias, alibi, out):
    turns = bank_turns()
    with ExitStack() as stack:
        def sb(name, shape, dt=F32):
            return stack.enter_context(nc.sbuf_tensor(name, shape, dt))

        sems = {}

        def sem(name):
            if name not in sems:
                sems[name] = stack.enter_context(nc.semaphore(name))
            return sems[name]

        q_stack = [sb(f"q_stack{p}", [SHIFT + 1, H, T], F32R) for p in range(2)]
        k_stack = [sb(f"k_stack{p}", [SHIFT + 1, H, T], F32R) for p in range(2)]
        xq_stack = sb("xq_stack", [SHIFT + 1, H, T], F32R)
        xk_stack = sb("xk_stack", [SHIFT + 1, H, 2, P], F32R)
        names = ["q", "k", "v", "o", "xq", "xk", "xv", "xo", "ffn"]
        w_hi = {n: sb(f"w_{n}_hi", [P, NB, D], F32R) for n in names}
        w_lo = {n: sb(f"w_{n}_lo", [P, NB, D], F32R) for n in names}
        probs = sb("probs", [P, 8, 3 * P])
        xprobs = sb("xprobs", [P, 8, T])
        self_t = sb("self_t", [P, 2, NB, T], F32R)
        chain_t = sb("chain_t", [P, 2, NB, T], F32R)
        ctx_t = sb("ctx_t", [P, 2, NB, 2, P], F32R)
        q_nat = sb("q_nat", [P, 2, NB, T])
        k_nat = sb("k_nat", [P, 2, NB, T])
        v_aug = [sb(f"v_aug{p}", [P, NB, H * VW + HD]) for p in range(2)]
        xv_aug = [sb(f"xv_aug{p}", [C, H * VW + HD]) for p in range(2)]
        heads_t = sb("heads_t", [P, 4, T])
        self_n = sb("self_n", [P, NB, D])
        chain_n = sb("chain_n", [P, NB, D])
        x_in = [sb(f"x_in{p}", [P, NB, D]) for p in range(2)]
        res = [sb(f"res{p}", [P, NB, D]) for p in range(2)]
        ctx_in = sb("ctx_in", [C, 2, D])
        bo = {n: sb(f"bias_{n}", [P, D]) for n in ("o", "xo", "ffn")}
        bcol = {n: sb(f"bias_{n}", [P, NB]) for n in ("q", "k", "v", "xq", "xk", "xv")}
        ident = sb("ident", [P, P])
        ident_b = sb("ident_b", [P, P], BF16)
        mask_q = sb("mask_q", [P, 4, P], BF16)
        mask_k = sb("mask_k", [P, 2, P], BF16)
        neg_max = {n: sb(f"neg_max_{n}", [P, NB, H]) for n in ("s", "x")}
        neg_max_t = {n: sb(f"neg_max_t_{n}", [NB * H, P]) for n in ("s", "x")}
        rsum = sb("rsum", [P, 2, H])
        half = sb("half", [P, NB])
        ln_sb = {n: (sb(f"st_{n}", [P, NB, 6]), sb(f"mv_{n}", [P, NB, 2]), sb(f"ve_{n}", [P, NB]),
                     sb(f"rstd_{n}", [P, NB]), sb(f"mr_{n}", [P, NB]), sb(f"nmr_{n}", [P, NB]))
                 for n in ("LN1", "LN2", "LN3")}

        banks = {r: [stack.enter_context(nc.psum_tensor(f"ps_{r}{i}", [P, 512], F32))
                     for i in range(n)] for r, n in RINGS.items()}
        scr = {n: nc.dram_tensor(f"scr_{n}", [2, D, T], F32, kind="Internal").ap()
               for n in ("q", "k", "xq", "xk")}

        def seq(i, c):
            return 2 * i + c

        def wait(eng, name, per, i, c, k=0):
            if isinstance(i, int):
                b = min(2 * i + c, LAST + 1)
                v = per * b + k
                if v > 0:
                    eng.wait_ge(sem(name), v)
            else:
                assert per * c + k > 0
                eng.wait_ge(sem(name), 2 * per * i + (per * c + k))
                if eng is nc.sync:
                    alone(eng)

        def alone(eng):
            eng.sem_inc(sem("waits_carried"), 1)

        def wait_pair(eng, name, per, i, pairs):
            if isinstance(i, int):
                v = per * min(i + pairs, NSEQ // 2)
                if v > 0:
                    eng.wait_ge(sem(name), v)
            else:
                assert pairs > 0
                eng.wait_ge(sem(name), per * i + per * pairs)
                if eng is nc.sync:
                    alone(eng)

        GIVEN_BACK = {
            "MAX": ("max_taken", 12), "XMAX": ("xmax_taken", 8),
            "SCORE": ("probs_ready", 16), "XSCORE": ("xprobs_ready", 8),
            "ATTEND": ("heads_taken", 2), "XATTEND": ("xheads_taken", 2),
            "HEADS_OUT": ("heads_normed", 2), "XHEADS_OUT": ("xheads_normed", 2),
            "LN1_T": ("LN1_T_lo", 1), "LN2_T": ("LN2_T_lo", 1), "LN3_T": ("LN3_T_lo", 1),
            "Q": ("Q_lo", 1), "K": ("K_lo", 1), "V": ("v_taken", 1), "XQ": ("XQ_lo", 1),
            "OUT_T": ("OUT_T_lo", 1), "XOUT_T": ("XOUT_T_lo", 1),
            "OUT_PROJ": ("res1_done", 1), "XOUT_PROJ": ("res2_done", 1),
            "MAX_T": ("max_t_taken", 1), "XMAX_T": ("xmax_t_taken", 1),
            "FFN": ("ffn_taken", 1), "XV": ("xv_taken", 1),
            "CTX_T": ("CTX_T_lo", 1), "XK": ("XK_lo", 1),
        }

        def bank_of(kind, i, c, part=0):
            return banks[FILLS[kind][0]][turns[kind, c, part][0]]

        def take_bank(eng, kind, i, c, part=0):
            bank, before = turns[kind, c, part]
            if before is not None:
                k0, b0, p0 = before
                name, per = GIVEN_BACK[k0]
                if k0 in ("CTX_T", "XK"):
                    wait_pair(eng, name, 1, i, b0 // 2 + 1)
                else:
                    wait(eng, name, per, i, b0, p0 + 1)
            return banks[FILLS[kind][0]][bank]

        def walk(eng, do):
            def step(i, t):
                for kind, b, part in step_order(t):
                    if kind in do:
                        do[kind](i, b, part)
            for t in range(FIRST_STEP, LOOP_FROM):
                step(0, t)
            with eng.Fori(0, (LOOP_TO - LOOP_FROM) // 2) as i:
                for t in range(LOOP_FROM, LOOP_FROM + 2):
                    step(i, t)
            for t in range(LOOP_TO, END_STEP):
                step(0, t)

        def blocks(tile, n=2):
            return tile[:, :].rearrange("p (a b) -> p a b", a=n)

        ws = ["q", "k", "v", "o", "xq", "xk", "xv", "xo"]
        raw_of = {}
        for n, nm in enumerate(ws[:6]):
            raw_of[nm] = probs[:, :, :].rearrange("p a b -> p (a b)")[:, n * 512:(n + 1) * 512]
        raw_of["xv"] = heads_t[:, 0:2, :].rearrange("p a b -> p (a b)")
        raw_of["xo"] = heads_t[:, 2:4, :].rearrange("p a b -> p (a b)")
        raw_of["f0"] = res[0][:, :, :].rearrange("p a b -> p (a b)")
        raw_of["f1"] = res[1][:, :, :].rearrange("p a b -> p (a b)")
        raw_of["f2"] = chain_n[:, :, :].rearrange("p a b -> p (a b)")
        raw = {n: v.rearrange("p (a b) -> p a b", a=NB) for n, v in raw_of.items()}
        xpf = xprobs[:, :, :].rearrange("p a b -> p (a b)")
        f1_t = xpf[:, 0:512].rearrange("p (a b) -> p a b", a=NB)
        f0_t = xpf[:, 512:1024].rearrange("p (a b) -> p a b", a=NB)
        f12 = xpf[:, 1024:1536].rearrange("p (a b) -> p a b", a=NB)
        PREP = ws + ["f1", "f0"]
        SCALE = {n: 1.0 for n in ws}
        SCALE["q"] = SCALE["xq"] = float(HD) ** -0.5

        block = stack.enter_context(nc.Block())

        @block.sync
        def _(sp):
            for n in PREP + ["f2"]:
                sp.dma_start(raw[n], wts[n].rearrange("(a p) c -> p a c", p=P)).then_inc(sem("w_loaded"), 16)
            for half_ in range(2):
                if half_:
                    sp.wait_ge(sem("alibi_copied"), 1)
                sp.dma_start(xpf[AUG:AUG + 2, :], alibi[:, half_ * 2048:(half_ + 1) * 2048]).then_inc(sem("alibi_loaded"), 16)
            for n in bcol:
                sp.dma_start(bcol[n][:, :], bias[n].rearrange("(a p) -> p a", p=P),
                             allow_slow_non_contiguous=True).then_inc(sem("b_loaded"), 16)
            for n in bo:
                sp.dma_start(bo[n][:, :], bias[n].rearrange("(a d) -> a d", a=1).broadcast_to([P, D])).then_inc(sem("b_loaded"), 16)
            sp.wait_ge(sem("pe_prep"), 12)
            sp.wait_ge(sem("prep_lo"), 9)

            def load_x(i, b, _):
                wait(sp, "res1_done", 1, i, b - 2, 1)
                sp.dma_start(x_in[b % 2][:, :, :], x[seq(i, b)].rearrange("(a p) d -> p a d", p=P))\
                    .then_inc(sem(f"x_loaded{b % 2}"), 16)

            def load_ctx(i, b, _):
                wait_pair(sp, "CTX_T_pe", 1, i, b // 2)
                sp.dma_start(ctx_in[:, :, :], ctx[bass.ds(seq(i, b), 2)].rearrange("s c d -> c s d"))\
                    .then_inc(sem("ctx_loaded"), 16)

            def save(name, nat):
                def f(i, b, _):
                    pair = name == "xk"
                    lo = {"q": "Q_lo", "k": "K_lo", "xq": "XQ_lo", "xk": "XK_lo"}[name]
                    if pair:
                        wait_pair(sp, lo, 1, i, b // 2 + 1)
                        wait(sp, "xk_stacked", 48, i, b)
                    else:
                        wait(sp, lo, 1, i, b, 1)
                        wait(sp, f"{name}_stacked", 48, i, b)
                    sp.dma_start(scr[name].rearrange("h (a p) t -> p (h a) t", p=P),
                                 nat[:, :, :, :].rearrange("p h a t -> p (h a) t"))\
                        .then_inc(sem(f"{name}_saved"), 16)
                return f

            def restack(name):
                parts = (0, 1, 0) if name.endswith("k") else (0, 0, 1)

                def f(i, b, _):
                    if name == "xk":
                        wait_pair(sp, "xk_saved", 16, i, b // 2 + 1)
                        wait(sp, "xscores_ready", 8, i, b - 1)
                    elif name == "xq":
                        wait(sp, "xq_saved", 16, i, b + 1)
                        wait(sp, "xscores_ready", 8, i, b)
                    else:
                        wait(sp, f"{name}_saved", 16, i, b + 1)
                        wait(sp, "scores_ready", 16, i, b - 1)
                    for n, half_ in enumerate(parts):
                        rows = scr[name][half_].rearrange("(h d) t -> d h t", d=HD)
                        if name == "xk":
                            dst = xk_stack[n * HD:(n + 1) * HD, :, b % 2, :]
                            rows = rows[:, :, (b % 2) * P:(b % 2 + 1) * P]
                        else:
                            dst = {"q": q_stack, "k": k_stack, "xq": [xq_stack] * 2}[name][b % 2][
                                n * HD:(n + 1) * HD, :, :]
                        sp.dma_start(dst.bitcast(F32), rows).then_inc(sem(f"{name}_stacked"), 16)
                return f

            def stack_max(which, dst_of):
                def f(i, b, _):
                    wait(sp, {"s": "max_t_taken", "x": "xmax_t_taken"}[which], 1, i, b, 1)
                    for qb in range(NB):
                        sp.dma_start(dst_of(b)[SHIFT:SHIFT + 1, :, qb * P:(qb + 1) * P].bitcast(F32),
                                     neg_max_t[which][qb * H:(qb + 1) * H, :])\
                            .then_inc(sem(f"{which}_shift_stacked"), 16)
                return f

            def store(i, b, _):
                wait(sp, "out_ready", 1, i, b, 1)
                sp.dma_start(out[seq(i, b)].rearrange("(a p) d -> p a d", p=P), res[b % 2][:, :, :])\
                    .then_inc(sem(f"stored{b % 2}"), 16)

            walk(sp, {
                "LOAD_X": load_x, "LOAD_CTX": load_ctx,
                "Q_SAVE": save("q", q_nat), "K_SAVE": save("k", k_nat),
                "XQ_SAVE": save("xq", q_nat), "XK_SAVE": save("xk", k_nat),
                "Q_STACK": restack("q"), "K_STACK": restack("k"),
                "XQ_STACK": restack("xq"), "XK_STACK": restack("xk"),
                "MAX_STACK": stack_max("s", lambda b: q_stack[b % 2]),
                "XMAX_STACK": stack_max("x", lambda b: xq_stack),
                "STORE": store,
            })
            for p in range(2):
                sp.wait_ge(sem(f"stored{p}"), 16 * NSEQ // 2)

        @block.tensor
        def _(pe):
            pe.wait_ge(sem("consts"), 4)
            pe.wait_ge(sem("w_loaded"), 16 * (len(PREP) + 1))
            for n, nm in enumerate(PREP):
                if n >= 2:
                    pe.wait_ge(sem("prep_lo"), n - 1)
                bk = blocks(banks["misc"][n % 2])
                for a in range(NB):
                    for k in range(NB):
                        mm = pe.transpose(bk[:, k, a * P:(a + 1) * P], raw[nm][:, a, k * P:(k + 1) * P],
                                          ident[:, :])
                mm.then_inc(sem("pe_prep"), 1)
            for stage, (lhs, rhs) in enumerate(((f1_t, raw["f2"]), (f0_t, f12))):
                pe.wait_ge(sem("prep_lo"), len(PREP) + stage)
                bk = blocks(banks["misc"][stage])
                for m in range(NB):
                    for k in range(NB):
                        mm = pe.matmul(bk[:, m, :], lhs[:, k, m * P:(m + 1) * P], rhs[:, k, :],
                                       start=(k == 0), stop=(k == NB - 1))
                mm.then_inc(sem("pe_prep"), 1)
            pe.wait_ge(sem("prep_lo"), len(PREP) + 2)
            pe.wait_ge(sem("stacks_set"), 1)

            def transposes(kind, src, ready, last):
                def f(i, b, _):
                    wait(pe, ready, 1, i, b, 1)
                    bk = blocks(take_bank(pe, kind, i, b))
                    for a in range(NB):
                        for k in range(NB):
                            mm = pe.transpose(bk[:, k, a * P:(a + 1) * P],
                                              src[:, a, k * P:(k + 1) * P], ident[:, :])
                    mm.then_inc(sem(f"{kind}_pe"), 1)
                return f

            def dims_out(kind, w, src_t, ready, pair=False):
                def f(i, b, _):
                    if pair:
                        wait_pair(pe, ready, 1, i, b // 2 + 1)
                    else:
                        wait(pe, ready, 1, i, b, 1)
                    bk = blocks(take_bank(pe, kind, i, b))
                    for m in range(NB):
                        for k in range(NB):
                            for n, (wt, h) in enumerate(((w_hi, 0), (w_hi, 1), (w_lo, 0))):
                                mm = pe.matmul(bk[:, m, :], wt[w][:, k, m * P:(m + 1) * P],
                                               src_t(h, k), start=(k == 0 and n == 0),
                                               stop=(k == NB - 1 and n == 2))
                    mm.then_inc(sem(f"{kind}_pe"), 1)
                return f

            def tokens_out(kind, w, src_t, ready):
                def f(i, b, _):
                    wait(pe, ready, 1, i, b, 1)
                    bk = blocks(take_bank(pe, kind, i, b))
                    for m in range(NB):
                        for k in range(NB):
                            for n, (h, wt) in enumerate(((0, w_hi), (0, w_lo), (1, w_hi))):
                                mm = pe.matmul(bk[:, m, :], src_t(h, k)[:, m * P:(m + 1) * P],
                                               wt[w][:, k, :], start=(k == 0 and n == 0),
                                               stop=(k == NB - 1 and n == 2))
                    mm.then_inc(sem(f"{kind}_pe"), 1)
                return f

            def context_values(i, b, _):
                wait_pair(pe, "CTX_T_lo", 1, i, b // 2 + 1)
                bk = take_bank(pe, "XV", i, b)
                for k in range(NB):
                    for n, (h, wt) in enumerate(((0, w_hi), (0, w_lo), (1, w_hi))):
                        mm = pe.matmul(bk[0:C, 0:D], ctx_t[:, h, k, b % 2, 0:C], wt["xv"][:, k, :],
                                       start=(k == 0 and n == 0), stop=(k == NB - 1 and n == 2))
                mm.then_inc(sem("XV_pe"), 1)

            def context_transposes(i, b, _):
                wait_pair(pe, "ctx_loaded", 16, i, b // 2 + 1)
                bk = take_bank(pe, "CTX_T", i, b)[:, :].rearrange("p (k s c) -> p k s c", k=NB, s=2)
                for s in range(2):
                    for k in range(NB):
                        mm = pe.transpose(bk[:, k, s, 0:C], ctx_in[:, s, k * P:(k + 1) * P],
                                          ident[0:C, 0:C])
                mm.then_inc(sem("CTX_T_pe"), 1)

            def narrow(ap):
                return ap.bitcast(BF16)[:, 1::2]

            def maxima(i, b, u):
                if u == 0:
                    wait(pe, "q_stacked", 48, i, b, 48)
                    wait(pe, "k_stacked", 48, i, b, 48)
                bk = take_bank(pe, "MAX", i, b, u)
                qs, ks = q_stack[b % 2], k_stack[b % 2]
                g, what = u // 3, u % 3
                if what == 0:
                    pe.matmul(bk[:, :], ident_b[:, :], mask_q[:, :, :].rearrange("p a b -> p (a b)"),
                              start=True, stop=False, skip_group_check=True)
                    for j in range(4):
                        mm = pe.matmul(bk[:, j * P:(j + 1) * P], narrow(qs[0:SHIFT, 4 * g + j, 0:P]),
                                       narrow(ks[0:SHIFT, 4 * g + j, 0:P]), start=False, stop=(j == 3),
                                       skip_group_check=True)
                else:
                    two = blocks(bk)
                    pe.matmul(two[:, :, P:T], ident_b[:, :], mask_q[:, 0:2, :],
                              start=True, stop=False, skip_group_check=True)
                    for j in range(2):
                        h = 4 * g + 2 * (what - 1) + j
                        mm = pe.matmul(two[:, j, :], narrow(qs[0:SHIFT, h, P:T]),
                                       narrow(ks[0:SHIFT, h, :]), start=False, stop=(j == 1),
                                       skip_group_check=True)
                mm.then_inc(sem("max_ready"), 1)

            def cross_maxima(i, b, u):
                if u == 0:
                    wait(pe, "xq_stacked", 48, i, b, 48)
                    wait(pe, "xk_stacked", 48, i, b, 48)
                bk = take_bank(pe, "XMAX", i, b, u)
                g, qb = u // 2, u % 2
                for j in range(4):
                    h = 4 * g + j
                    mm = pe.matmul(bk[:, j * C:(j + 1) * C], narrow(xq_stack[0:SHIFT, h, qb * P:(qb + 1) * P]),
                                   narrow(xk_stack[0:SHIFT, h, b % 2, 0:C]), start=True, stop=True)
                mm.then_inc(sem("xmax_ready"), 1)

            def max_transpose(kind, which, taken, per):
                def f(i, b, _):
                    wait(pe, taken, per, i, b, per)
                    bk = take_bank(pe, kind, i, b)
                    pe.transpose(bk[0:NB * H, 0:P], neg_max[which][:, :, :].rearrange("p a h -> p (a h)"),
                                 ident[:, :]).then_inc(sem(f"{kind}_pe"), 1)
                return f

            def scores(i, b, h):
                if h == 0:
                    wait(pe, "s_shift_stacked", 32, i, b, 32)
                bk = take_bank(pe, "SCORE", i, b, h)
                qs, ks = q_stack[b % 2], k_stack[b % 2]
                pe.matmul(bk[:, P:3 * P], ident_b[:, :], mask_k[:, :, :].rearrange("p a b -> p (a b)"),
                          start=True, stop=False, skip_group_check=True)
                pe.matmul(bk[:, 0:T], ks[:, h, P:T], qs[:, h, :], start=False, stop=False,
                          skip_group_check=True)
                pe.matmul(bk[:, T:2 * T], ks[:, h, 0:P], qs[:, h, :], start=False, stop=True,
                          skip_group_check=True).then_inc(sem("scores_ready"), 1)

            def cross_scores(i, b, u):
                if u == 0:
                    wait(pe, "x_shift_stacked", 32, i, b, 32)
                bk = take_bank(pe, "XSCORE", i, b, u)
                for j in range(2):
                    h = 2 * u + j
                    mm = pe.matmul(bk[0:C, j * T:(j + 1) * T], xk_stack[:, h, b % 2, 0:C],
                                   xq_stack[:, h, :], start=True, stop=True)
                mm.then_inc(sem("xscores_ready"), 1)

            def attend(i, b, g):
                if g == 0:
                    wait(pe, "v_taken", 1, i, b, 1)
                if g % 2 == 0:
                    take_bank(pe, "ATTEND", i, b, g // 2)
                bk = banks["attend"][0]
                wait(pe, "probs_ready", 16, i, b, 4 * g + 4)
                at = (g % 2) * T
                for j in range(4):
                    h = 4 * g + j
                    pe.matmul(bk[32 * j:32 * j + 32, at:at + T], v_aug[b % 2][:, 0, h * VW:h * VW + 32],
                              probs[:, h % 8, P:3 * P], start=True, stop=False, skip_group_check=True)
                for j in range(4):
                    h = 4 * g + j
                    mm = pe.matmul(bk[32 * j:32 * j + 32, at + P:at + T],
                                   v_aug[b % 2][:, 1, h * VW:h * VW + 32], probs[:, h % 8, 0:P],
                                   start=False, stop=True, skip_group_check=True)
                mm.then_inc(sem("attended"), 1)

            def cross_attend(i, b, g):
                if g == 0:
                    wait(pe, "xv_taken", 1, i, b, 1)
                if g % 2 == 0:
                    take_bank(pe, "XATTEND", i, b, g // 2)
                bk = banks["attend"][0]
                wait(pe, "xprobs_ready", 8, i, b, 2 * g + 2)
                at = (g % 2) * T
                for j in range(4):
                    h = 4 * g + j
                    mm = pe.matmul(bk[32 * j:32 * j + 32, at:at + T], xv_aug[b % 2][:, h * VW:h * VW + 32],
                                   xprobs[0:C, h % 8, :], start=True, stop=True, skip_group_check=True)
                mm.then_inc(sem("xattended"), 1)

            def heads_out(kind, taken):
                def f(i, b, qb):
                    if qb == 0:
                        wait(pe, taken, 2, i, b, 2)
                    bk = take_bank(pe, kind, i, b, qb)
                    for g in range(4):
                        mm = pe.transpose(bk[:, g * P:(g + 1) * P], heads_t[:, g, qb * P:(qb + 1) * P],
                                          ident[:, :])
                    mm.then_inc(sem(f"{kind}_pe"), 1)
                return f

            self_of = lambda h, k: self_t[:, h, k, :]
            chain_of = lambda h, k: chain_t[:, h, k, :]
            ctx_of = lambda h, k: ctx_t[:, h, k, :, :].rearrange("p s c -> p (s c)")

            def norm_transposes(kind, normed):
                def f(i, b, _):
                    wait(pe, normed, 2, i, b, 2)
                    bk = blocks(take_bank(pe, kind, i, b))
                    for a in range(NB):
                        for k in range(NB):
                            mm = pe.transpose(bk[:, k, a * P:(a + 1) * P],
                                              chain_n[:, a, k * P:(k + 1) * P], ident[:, :])
                    mm.then_inc(sem(f"{kind}_pe"), 1)
                return f

            walk(pe, {
                "LN1_T": transposes("LN1_T", self_n, "LN1_done", None),
                "LN2_T": transposes("LN2_T", chain_n, "LN2_done", None),
                "LN3_T": transposes("LN3_T", chain_n, "LN3_done", None),
                "OUT_T": norm_transposes("OUT_T", "heads_normed"),
                "XOUT_T": norm_transposes("XOUT_T", "xheads_normed"),
                "Q": dims_out("Q", "q", self_of, "LN1_T_lo"),
                "K": dims_out("K", "k", self_of, "LN1_T_lo"),
                "V": tokens_out("V", "v", self_of, "LN1_T_lo"),
                "XQ": dims_out("XQ", "xq", chain_of, "LN2_T_lo"),
                "XK": dims_out("XK", "xk", ctx_of, "CTX_T_lo", pair=True),
                "XV": context_values,
                "CTX_T": context_transposes,
                "OUT_PROJ": tokens_out("OUT_PROJ", "o", chain_of, "OUT_T_lo"),
                "XOUT_PROJ": tokens_out("XOUT_PROJ", "xo", chain_of, "XOUT_T_lo"),
                "FFN": tokens_out("FFN", "ffn", chain_of, "LN3_T_lo"),
                "MAX": maxima, "XMAX": cross_maxima,
                "MAX_T": max_transpose("MAX_T", "s", "max_taken", 12),
                "XMAX_T": max_transpose("XMAX_T", "x", "xmax_taken", 8),
                "SCORE": scores, "XSCORE": cross_scores,
                "ATTEND": attend, "XATTEND": cross_attend,
                "HEADS_OUT": heads_out("HEADS_OUT", "heads_taken"),
                "XHEADS_OUT": heads_out("XHEADS_OUT", "xheads_taken"),
            })

        SPLITS = {
            "LN1_T": (None, self_t), "LN2_T": (None, chain_t), "LN3_T": (None, chain_t),
            "OUT_T": ("v", chain_t), "XOUT_T": ("xv", chain_t),
            "Q": ("q", q_nat), "K": ("k", k_nat), "XQ": ("xq", q_nat), "XK": ("xk", k_nat),
            "CTX_T": (None, ctx_t),
        }

        @block.scalar
        def _(act):
            for n, nm in enumerate(PREP):
                act.wait_ge(sem("pe_prep"), n + 1)
                bk = blocks(banks["misc"][n % 2])
                if nm in SCALE:
                    act.activation(w_hi[nm][:, :, :], bk, ACT.Copy, scale=SCALE[nm]).then_inc(sem("prep_hi"), 1)
                else:
                    act.activation({"f1": f1_t, "f0": f0_t}[nm], bk, ACT.Copy).then_inc(sem("prep_hi"), 1)
            act.wait_ge(sem("pe_prep"), len(PREP) + 1)
            act.activation(f12, blocks(banks["misc"][0]), ACT.Copy).then_inc(sem("prep_hi"), 1)
            act.wait_ge(sem("pe_prep"), len(PREP) + 2)
            act.activation(w_hi["ffn"][:, :, :], blocks(banks["misc"][1]), ACT.Copy).then_inc(sem("prep_hi"), 1)
            act.wait_ge(sem("b_loaded"), 16 * 9)
            act.wait_ge(sem("b_scaled"), 1)

            def hi(kind, free):
                bias_of, dst = SPLITS[kind]

                def f(i, b, _):
                    if kind in ("CTX_T", "XK"):
                        wait_pair(act, f"{kind}_pe", 1, i, b // 2 + 1)
                    else:
                        wait(act, f"{kind}_pe", 1, i, b, 1)
                    free(i, b)
                    bk = blocks(bank_of(kind, i, b))
                    if kind == "CTX_T":
                        act.activation(dst[:, 0, :, :, 0:C].rearrange("p a s c -> p (a s) c"),
                                       bank_of(kind, i, b)[:, :].rearrange("p (a c) -> p a c", a=4)[:, :, 0:C],
                                       ACT.Copy).then_inc(sem(f"{kind}_hi"), 1)
                    elif bias_of is None:
                        act.activation(dst[:, 0, :, :], bk, ACT.Copy).then_inc(sem(f"{kind}_hi"), 1)
                    else:
                        for k in range(NB):
                            o = dst[:, 0, k, :]
                            if dst is q_nat or dst is k_nat:
                                o = o.bitcast(F32R)
                            last = act.activation(o, bk[:, k, :], ACT.Identity, bias=bcol[bias_of][:, k:k + 1])
                        last.then_inc(sem(f"{kind}_hi"), 1)
                return f

            def exp_self(i, b, h):
                wait(act, "scores_ready", 16, i, b, h + 1)
                wait(act, "attended", 4, i, b, h // 4 - 1)
                act.activation(probs[:, h % 8, :], bank_of("SCORE", i, b, h)[:, P:4 * P], ACT.Exp)\
                    .then_inc(sem("probs_ready"), 1)

            def exp_cross(i, b, u):
                wait(act, "xscores_ready", 8, i, b, u + 1)
                wait(act, "xattended", 4, i, b, u // 2 - 1)
                at = 2 * u % 8
                act.activation(xprobs[0:C, at:at + 2, :], blocks(bank_of("XSCORE", i, b, u))[0:C],
                               ACT.Exp).then_inc(sem("xprobs_ready"), 1)

            def take_heads(kind, ready, other, ahead):
                def f(i, b, g):
                    if g % 2 == 0:
                        return
                    wait(act, ready, 4, i, b, g + 1)
                    if g == 1:
                        wait(act, other, 2, i, b + ahead, 0)
                    act.activation(heads_t[:, g - 1:g + 1, :], blocks(banks["attend"][0]), ACT.Copy)\
                        .then_inc(sem({"ATTEND": "heads_taken", "XATTEND": "xheads_taken"}[kind]), 1)
                return f

            def take_v(i, b, _):
                wait(act, "V_pe", 1, i, b, 1)
                wait(act, "attended", 4, i, b - 1)
                act.activation(v_aug[b % 2][:, :, 0:H * VW].rearrange("p a (h w) -> p a h w", w=VW)[:, :, :, 0:HD],
                               bank_of("V", i, b)[:, :].rearrange("p (a h w) -> p a h w", a=NB, w=HD),
                               ACT.Copy).then_inc(sem("v_taken"), 1)

            def take_xv(i, b, _):
                wait(act, "XV_pe", 1, i, b, 1)
                wait(act, "xattended", 4, i, b - 1)
                act.activation(xv_aug[b % 2][:, 0:H * VW].rearrange("p (h w) -> p h w", w=VW)[:, :, 0:HD],
                               bank_of("XV", i, b)[0:C, 0:D].rearrange("p (h w) -> p h w", w=HD),
                               ACT.Copy).then_inc(sem("xv_taken"), 1)

            def take_max_t(kind, which, stacked, taken):
                def f(i, b, _):
                    wait(act, f"{kind}_pe", 1, i, b, 1)
                    wait(act, stacked, 32, i, b)
                    act.activation(neg_max_t[which][:, :].bitcast(F32R), bank_of(kind, i, b)[0:NB * H, 0:P],
                                   ACT.Copy).then_inc(sem(taken), 1)
                return f

            def tanh(i, b, _):
                wait(act, "ffn_taken", 1, i, b, 1)
                act.activation(chain_n[:, :, :], chain_n[:, :, :], ACT.Tanh).then_inc(sem("tanh_done"), 1)

            def k_free(i, b):
                wait_pair(act, "xk_saved", 16, i, b // 2)

            walk(act, {
                "LN1_T": hi("LN1_T", lambda i, b: wait(act, "V_pe", 1, i, b)),
                "LN2_T": hi("LN2_T", lambda i, b: None),
                "LN3_T": hi("LN3_T", lambda i, b: None),
                "OUT_T": hi("OUT_T", lambda i, b: wait(act, "FFN_pe", 1, i, b - 1)),
                "XOUT_T": hi("XOUT_T", lambda i, b: wait(act, "XQ_pe", 1, i, b + 2)),
                "CTX_T": hi("CTX_T", lambda i, b: wait(act, "XV_pe", 1, i, b)),
                "Q": hi("Q", lambda i, b: wait(act, "xq_saved", 16, i, b - 1)),
                "XQ": hi("XQ", lambda i, b: wait(act, "q_saved", 16, i, b + 2)),
                "K": hi("K", k_free),
                "XK": hi("XK", lambda i, b: wait(act, "k_saved", 16, i, b + 2)),
                "V": take_v, "XV": take_xv,
                "SCORE": exp_self, "XSCORE": exp_cross,
                "ATTEND": take_heads("ATTEND", "attended", "XHEADS_OUT_pe", -1),
                "XATTEND": take_heads("XATTEND", "xattended", "HEADS_OUT_pe", 2),
                "MAX_T": take_max_t("MAX_T", "s", "s_shift_stacked", "max_t_taken"),
                "XMAX_T": take_max_t("XMAX_T", "x", "x_shift_stacked", "xmax_t_taken"),
                "FFN": tanh,
            })

        @block.vector
        def _(dve):
            dve.memset(half[:, :], -0.5)
            for p in range(2):
                dve.memset(v_aug[p][:, :, :], 1.0)
                dve.memset(xv_aug[p][:, :], 1.0)
                for st in (q_stack[p], k_stack[p]):
                    dve.memset(st[:, :, :].bitcast(F32), 0.0)
            dve.memset(xk_stack[:, :, :, :].bitcast(F32), 0.0)
            dve.memset(ctx_t[:, :, :, :, :].bitcast(F32), 0.0)
            dve.memset(xq_stack[:, :, :].bitcast(F32), 0.0).then_inc(sem("zeroed"), 1)
            dve.wait_ge(sem("zeroed"), 1)
            for p in range(2):
                dve.memset(q_stack[p][AUG:AUG + 2, :, :].bitcast(F32), 1.0)
                dve.memset(k_stack[p][SHIFT:SHIFT + 1, :, :].bitcast(F32), 1.0)
            dve.memset(xk_stack[SHIFT:SHIFT + 1, :, :, :].bitcast(F32), 1.0)
            for half_ in range(2):
                dve.wait_ge(sem("alibi_loaded"), 16 * (half_ + 1))
                for p in range(2):
                    last = dve.tensor_copy(
                        k_stack[p][AUG:AUG + 2, half_ * 8:half_ * 8 + 8, :].rearrange("p h t -> p (h t)"),
                        xpf[AUG:AUG + 2, :])
                last.then_inc(sem("alibi_copied"), 1)
            dve.wait_ge(sem("b_loaded"), 16 * 9)
            dve.tensor_scalar(bcol["q"][:, :], bcol["q"][:, :], SCALE["q"], None, ALU.mult)
            dve.tensor_scalar(bcol["xq"][:, :], bcol["xq"][:, :], SCALE["xq"], None, ALU.mult)\
                .then_inc(sem("b_scaled"), 1)
            dve.wait_ge(sem("alibi_copied"), 2)
            dve.engine_nop().then_inc(sem("stacks_set"), 1)
            for n, nm in enumerate(PREP + ["f12", "ffn"]):
                dve.wait_ge(sem("prep_hi"), n + 1)
                if nm in SCALE or nm == "ffn":
                    bk = blocks(banks["misc"][n % 2])
                    dve.scalar_tensor_tensor(out=w_lo[nm][:, :, :], in0=bk, scalar=SCALE.get(nm, 1.0),
                                             in1=w_hi[nm][:, :, :].bitcast(F32), op0=ALU.mult,
                                             op1=ALU.subtract).then_inc(sem("prep_lo"), 1)
                else:
                    dve.engine_nop().then_inc(sem("prep_lo"), 1)

            def lo(kind):
                bias_of, dst = SPLITS[kind]

                def f(i, b, _):
                    if kind in ("CTX_T", "XK"):
                        wait_pair(dve, f"{kind}_hi", 1, i, b // 2 + 1)
                    else:
                        wait(dve, f"{kind}_hi", 1, i, b, 1)
                    bk = blocks(bank_of(kind, i, b))
                    if kind == "CTX_T":
                        v = lambda h: dst[:, h, :, :, 0:C].rearrange("p a s c -> p (a s) c")
                        last = dve.tensor_tensor(
                            v(1), bank_of(kind, i, b)[:, :].rearrange("p (a c) -> p a c", a=4)[:, :, 0:C],
                            v(0).bitcast(F32), ALU.subtract)
                    elif bias_of is None:
                        last = dve.tensor_tensor(dst[:, 1, :, :], bk, dst[:, 0, :, :].bitcast(F32), ALU.subtract)
                    else:
                        for k in range(NB):
                            o = dst[:, 1, k, :]
                            if dst is q_nat or dst is k_nat:
                                o = o.bitcast(F32R)
                            last = dve.scalar_tensor_tensor(
                                out=o, in0=bk[:, k, :], scalar=bcol[bias_of][:, k:k + 1],
                                in1=dst[:, 0, k, :].bitcast(F32), op0=ALU.add, op1=ALU.subtract)
                    last.then_inc(sem(f"{kind}_lo"), 1)
                return f

            def maxima(i, b, u):
                wait(dve, "max_ready", 12, i, b, u + 1)
                if u == 0:
                    wait(dve, "MAX_T_pe", 1, i, b)
                g, what = u // 3, u % 3
                bk = bank_of("MAX", i, b, u)
                if what == 0:
                    ins, o = blocks(bk, 4), neg_max["s"][:, 0, 4 * g:4 * g + 4]
                else:
                    h = 4 * g + 2 * (what - 1)
                    ins, o = blocks(bk), neg_max["s"][:, 1, h:h + 2]
                dve.tensor_reduce(o, ins, AX.X, ALU.max, negate=True).then_inc(sem("max_taken"), 1)

            def cross_maxima(i, b, u):
                wait(dve, "xmax_ready", 8, i, b, u + 1)
                if u == 0:
                    wait(dve, "XMAX_T_pe", 1, i, b)
                g, qb = u // 2, u % 2
                bk = bank_of("XMAX", i, b, u)[:, 0:4 * C].rearrange("p (a c) -> p a c", a=4)
                dve.tensor_reduce(neg_max["x"][:, qb, 4 * g:4 * g + 4], bk, AX.X, ALU.max,
                                  negate=True).then_inc(sem("xmax_taken"), 1)

            def moments(kind, src, ready):
                st, mv = ln_sb[kind][0:2]

                def f(i, b, _):
                    ready(i, b)
                    wait(dve, f"{kind}_done", 1, i, b)
                    for a in range(NB):
                        dve.bn_stats(st[:, a, :], src[b % 2][:, a, :]).then_inc(sem(f"{kind}_stats"), 1)
                    wait(dve, f"{kind}_stats", 2, i, b, 2)
                    alone(dve)
                    for a in range(NB):
                        last = dve.bn_aggr(mv[:, a, :], st[:, a, :])
                    last.then_inc(sem(f"{kind}_moments"), 1)
                return f

            def x_ready(i, b):
                wait_x(dve, i, b)

            def wait_x(eng, i, b):
                v = 16 * (b // 2 + 1)
                eng.wait_ge(sem(f"x_loaded{b % 2}"), v if isinstance(i, int) else 16 * i + v)

            def norm_heads(kind, done, free):
                def f(i, b, qb):
                    wait(dve, f"{kind}_pe", 2, i, b, qb + 1)
                    if qb == 0:
                        free(i, b)
                    bk = bank_of(kind, i, b, qb)[:, :].rearrange("p (h w) -> p h w", w=32)
                    rs = rsum[:, qb, :]
                    dve.reciprocal(rs.unsqueeze(2), bk[:, :, HD:HD + 1]).then_inc(sem(f"{kind}_rsum"), 1)
                    wait(dve, f"{kind}_rsum", 2, i, b, qb + 1)
                    dve.tensor_tensor(chain_n[:, qb, :].rearrange("p (h w) -> p h w", w=HD),
                                      bk[:, :, 0:HD], rs.unsqueeze(2).to_broadcast([P, H, HD]),
                                      ALU.mult).then_inc(sem(done), 1)
                return f

            def residual1(i, b, _):
                wait(dve, "OUT_PROJ_pe", 1, i, b, 1)
                wait(dve, "x_biased", 1, i, b, 1)
                v = 16 * (b // 2)
                if not isinstance(i, int) or v > 0:
                    dve.wait_ge(sem(f"stored{b % 2}"), v if isinstance(i, int) else 16 * i + v)
                dve.tensor_tensor(res[b % 2][:, :, :], blocks(bank_of("OUT_PROJ", i, b)),
                                  x_in[b % 2][:, :, :], ALU.add).then_inc(sem("res1_done"), 1)

            def residual2(i, b, _):
                wait(dve, "XOUT_PROJ_pe", 1, i, b, 1)
                wait(dve, "res_biased", 1, i, b, 1)
                dve.tensor_tensor(res[b % 2][:, :, :], blocks(bank_of("XOUT_PROJ", i, b)),
                                  res[b % 2][:, :, :], ALU.add).then_inc(sem("res2_done"), 1)

            def ffn_bias(i, b, _):
                wait(dve, "FFN_pe", 1, i, b, 1)
                bk = blocks(bank_of("FFN", i, b))
                dve.tensor_tensor(chain_n[:, :, :], bk,
                                  bo["ffn"][:, :].unsqueeze(1).to_broadcast([P, NB, D]), ALU.add)\
                    .then_inc(sem("ffn_taken"), 1)

            do = {k: lo(k) for k in SPLITS}
            do.update({
                "MAX": maxima, "XMAX": cross_maxima,
                "LN1": moments("LN1", x_in, x_ready),
                "LN2": moments("LN2", res, lambda i, b: wait(dve, "res1_done", 1, i, b, 1)),
                "LN3": moments("LN3", res, lambda i, b: wait(dve, "res2_done", 1, i, b, 1)),
                "HEADS_OUT": norm_heads("HEADS_OUT", "heads_normed",
                                        lambda i, b: wait(dve, "out_ready", 1, i, b - 1)),
                "XHEADS_OUT": norm_heads("XHEADS_OUT", "xheads_normed",
                                         lambda i, b: wait(dve, "LN2_T_pe", 1, i, b + 2)),
                "OUT_PROJ": residual1, "XOUT_PROJ": residual2, "FFN": ffn_bias,
            })
            walk(dve, do)

        @block.gpsimd
        def _(pool):
            pool.memset(ident[:, :], 0.0).then_inc(sem("const0"), 1)
            pool.memset(ident_b[:, :], 0.0).then_inc(sem("const0"), 1)
            pool.memset(mask_q[:, :, :], 0.0).then_inc(sem("const0"), 1)
            pool.memset(mask_k[:, :, :], 0.0).then_inc(sem("const0"), 1)
            pool.wait_ge(sem("const0"), 4)
            for m in (ident, ident_b):
                pool.affine_select(out=m[:, :], in_=m[:, :], compare_op=ALU.not_equal, fill=1.0, base=0,
                                   pattern=[[-1, P]], channel_multiplier=1).then_inc(sem("consts"), 1)
            pool.affine_select(out=mask_q[:, :, :], in_=mask_q[:, :, :], compare_op=ALU.is_ge, fill=BIG,
                               base=0, pattern=[[0, 4], [-1, P]], channel_multiplier=1)\
                .then_inc(sem("consts"), 1)
            pool.affine_select(out=mask_k[:, :, :], in_=mask_k[:, :, :], compare_op=ALU.is_ge, fill=BIG,
                               base=0, pattern=[[0, 2], [1, P]], channel_multiplier=-1)\
                .then_inc(sem("consts"), 1)
            pool.wait_ge(sem("b_loaded"), 16 * 9)
            pool.wait_ge(sem("zeroed"), 1)

            def normalise(kind, src, dst, free, bias_name, biased):
                st, mv, ve, rstd, mr, nmr = ln_sb[kind]

                def f(i, b, _):
                    wait(pool, f"{kind}_moments", 1, i, b, 1)
                    alone(pool)
                    s = f"{kind}_small"
                    pool.tensor_scalar(ve[:, :].unsqueeze(2), mv[:, :, 1:2], 1.0, EPS, ALU.mult, ALU.add)\
                        .then_inc(sem(s), 1)
                    wait(pool, s, 4, i, b, 1)
                    pool.tensor_tensor(rstd[:, :], ve[:, :], half[:, :], ALU.pow).then_inc(sem(s), 1)
                    wait(pool, s, 4, i, b, 2)
                    pool.tensor_tensor(mr[:, :].unsqueeze(2), mv[:, :, 0:1], rstd[:, :].unsqueeze(2), ALU.mult)\
                        .then_inc(sem(s), 1)
                    wait(pool, s, 4, i, b, 3)
                    alone(pool)
                    pool.tensor_scalar(nmr[:, :], mr[:, :], -1.0, 0.0, ALU.mult, ALU.add).then_inc(sem(s), 1)
                    wait(pool, s, 4, i, b, 4)
                    free(i, b)
                    alone(pool)
                    for a in range(NB):
                        last = pool.tensor_scalar(dst[:, a, :], src[b % 2][:, a, :], rstd[:, a:a + 1],
                                                  nmr[:, a:a + 1], ALU.mult, ALU.add)
                    last.then_inc(sem(f"{kind}_done"), 1)
                    if bias_name:
                        wait(pool, f"{kind}_done", 1, i, b, 1)
                        pool.tensor_tensor(src[b % 2][:, :, :], src[b % 2][:, :, :],
                                           bo[bias_name][:, :].unsqueeze(1).to_broadcast([P, NB, D]),
                                           ALU.add).then_inc(sem(biased), 1)
                return f

            def finish(i, b, _):
                wait(pool, "tanh_done", 1, i, b, 1)
                pool.tensor_tensor(res[b % 2][:, :, :], res[b % 2][:, :, :], chain_n[:, :, :], ALU.add)\
                    .then_inc(sem("out_ready"), 1)

            walk(pool, {
                "LN1": normalise("LN1", x_in, self_n, lambda i, b: wait(pool, "LN1_T_pe", 1, i, b),
                                 "o", "x_biased"),
                "LN2": normalise("LN2", res, chain_n, lambda i, b: None, "xo", "res_biased"),
                "LN3": normalise("LN3", res, chain_n, lambda i, b: None, None, None),
                "FFN": finish,
            })



def alibi_rows():
    slopes = (2.0 ** (-8.0 * np.arange(1, H + 1, dtype=np.float64) / H)).astype(np.float32)
    v = slopes.astype(np.float64)[:, None] * (np.arange(T, dtype=np.float64) - T // 2)[None, :]
    top = np.exp2(np.floor(np.log2(np.maximum(np.abs(v), 1e-30))))
    hi = np.round(v / top * 2048) / 2048 * top
    return np.stack([hi, v - hi]).astype(np.float32).reshape(2, H * T)


def kernel(x, ctx_1024, L0_attn_Wq, L0_attn_bq, L0_attn_Wk, L0_attn_bk, L0_attn_Wv, L0_attn_bv,
           L0_attn_Wo, L0_attn_bo, L0_xattn_Wq, L0_xattn_bq, L0_xattn_Wk, L0_xattn_bk, L0_xattn_Wv,
           L0_xattn_bv, L0_xattn_Wo, L0_xattn_bo, L0_ffn_weight, L0_ffn_aux_weight1,
           L0_ffn_aux_weight2, L0_ffn_bias):
    import concourse.bacc as bacc
    from concourse.bass_utils import run_bass_kernel_spmd

    given = {
        "x": x, "ctx": ctx_1024, "w_q": L0_attn_Wq, "w_k": L0_attn_Wk, "w_v": L0_attn_Wv,
        "w_o": L0_attn_Wo, "w_xq": L0_xattn_Wq, "w_xk": L0_xattn_Wk, "w_xv": L0_xattn_Wv,
        "w_xo": L0_xattn_Wo, "w_f0": L0_ffn_weight, "w_f1": L0_ffn_aux_weight1,
        "w_f2": L0_ffn_aux_weight2, "b_q": L0_attn_bq, "b_k": L0_attn_bk, "b_v": L0_attn_bv,
        "b_o": L0_attn_bo, "b_xq": L0_xattn_bq, "b_xk": L0_xattn_bk, "b_xv": L0_xattn_bv,
        "b_xo": L0_xattn_bo, "b_ffn": L0_ffn_bias, "alibi": alibi_rows(),
    }
    nc = bacc.Bacc("TRN2", target_bir_lowering=False, num_devices=1)
    arrays, aps = {}, {}
    for name, value in given.items():
        a = np.ascontiguousarray(value)
        arrays[f"in_{name}"] = a
        aps[name] = nc.dram_tensor(f"in_{name}", a.shape, mybir.dt.from_np(a.dtype),
                                   kind="ExternalInput").ap()
    out = nc.dram_tensor("out_y", (NSEQ, T, D), F32, kind="ExternalOutput").ap()
    build(nc, aps["x"], aps["ctx"], {n[2:]: v for n, v in aps.items() if n.startswith("w_")},
          {n[2:]: v for n, v in aps.items() if n.startswith("b_")}, aps["alibi"], out)
    r = run_bass_kernel_spmd(nc, [arrays], core_ids=[0])
    return r.results[0]["out_y"]
```

```python
from contextlib import ExitStack

import numpy as np

import concourse.bass as bass
from concourse import mybir

F32 = mybir.dt.float32
F32R = mybir.dt.float32r
BF16 = mybir.dt.bfloat16
ALU = mybir.AluOpType
ACT = mybir.ActivationFunctionType
AX = mybir.AxisListType

P = 128
NSEQ = 64
T = 256
D = 256
H = 16
HD = D // H
C = 120
NB = D // P
VW = HD + 1
AUG = 64
SHIFT = 96
EPS = 1e-5
BIG = -1e30
LAST = NSEQ - 1



ORDER = {
    "SP": (
        ("STORE", -3, 0), ("XMAX_STACK", -2, 0), ("LOAD_X", 1, 0), ("XK_STACK", -1, 0),
        ("MAX_STACK", 0, 0), ("XQ_SAVE", -1, 0), ("LOAD_CTX", 0, 0), ("XQ_STACK", -1, 0),
        ("K_SAVE", 1, 0), ("Q_SAVE", 1, 0), ("K_STACK", 1, 0), ("Q_STACK", 1, 0), ("XK_SAVE", 0, 0),
    ),
    "PE": (
        ("SCORE", -1, 11), ("ATTEND", -1, 1), ("SCORE", -1, 12), ("SCORE", -1, 13),
        ("LN3_T", -3, 0), ("XMAX", -2, 3), ("ATTEND", -1, 2), ("SCORE", -1, 14), ("XMAX", -2, 4),
        ("SCORE", -1, 15), ("XMAX", -2, 5), ("FFN", -3, 0), ("ATTEND", -1, 3), ("XMAX", -2, 6),
        ("V", 0, 0), ("XMAX", -2, 7), ("HEADS_OUT", -1, 0), ("HEADS_OUT", -1, 1), ("MAX", 0, 0),
        ("XMAX_T", -2, 0), ("MAX", 0, 1), ("OUT_T", -1, 0), ("MAX", 0, 2), ("XV", -1, 0),
        ("MAX", 0, 3), ("MAX", 0, 4), ("MAX", 0, 5), ("OUT_PROJ", -1, 0), ("XSCORE", -2, 0),
        ("XSCORE", -2, 1), ("MAX", 0, 6), ("MAX", 0, 7), ("XSCORE", -2, 2), ("MAX", 0, 8),
        ("XSCORE", -2, 3), ("XATTEND", -2, 0), ("XSCORE", -2, 4), ("MAX", 0, 9), ("XSCORE", -2, 5),
        ("XATTEND", -2, 1), ("MAX", 0, 10), ("XSCORE", -2, 6), ("MAX", 0, 11), ("XSCORE", -2, 7),
        ("LN2_T", -1, 0), ("MAX_T", 0, 0), ("XATTEND", -2, 2), ("XATTEND", -2, 3), ("XQ", -1, 0),
        ("SCORE", 0, 0), ("SCORE", 0, 1), ("XHEADS_OUT", -2, 0), ("SCORE", 0, 2),
        ("XHEADS_OUT", -2, 1), ("SCORE", 0, 3), ("LN1_T", 1, 0), ("SCORE", 0, 4), ("XOUT_T", -2, 0),
        ("ATTEND", 0, 0), ("SCORE", 0, 5), ("K", 1, 0), ("SCORE", 0, 6), ("XOUT_PROJ", -2, 0),
        ("SCORE", 0, 7), ("SCORE", 0, 8), ("CTX_T", 0, 0), ("Q", 1, 0), ("SCORE", 0, 9),
        ("XMAX", -1, 0), ("SCORE", 0, 10), ("XMAX", -1, 1), ("XK", 0, 0), ("XMAX", -1, 2),
    ),
    "ACT": (
        ("SCORE", -1, 11), ("ATTEND", -1, 1), ("SCORE", -1, 12), ("SCORE", -1, 13),
        ("LN3_T", -3, 0), ("SCORE", -1, 14), ("SCORE", -1, 15), ("FFN", -3, 0), ("ATTEND", -1, 3),
        ("V", 0, 0), ("XMAX_T", -2, 0), ("OUT_T", -1, 0), ("XSCORE", -2, 0), ("XSCORE", -2, 1),
        ("XV", -1, 0), ("XSCORE", -2, 2), ("XSCORE", -2, 3), ("XSCORE", -2, 4), ("XSCORE", -2, 5),
        ("XATTEND", -2, 1), ("XSCORE", -2, 6), ("XSCORE", -2, 7), ("LN2_T", -1, 0), ("MAX_T", 0, 0),
        ("XATTEND", -2, 3), ("XQ", -1, 0), ("SCORE", 0, 0), ("SCORE", 0, 1), ("SCORE", 0, 2),
        ("SCORE", 0, 3), ("LN1_T", 1, 0), ("SCORE", 0, 4), ("XOUT_T", -2, 0), ("K", 1, 0),
        ("SCORE", 0, 5), ("SCORE", 0, 6), ("CTX_T", 0, 0), ("SCORE", 0, 7), ("SCORE", 0, 8),
        ("Q", 1, 0), ("SCORE", 0, 9), ("SCORE", 0, 10), ("XK", 0, 0),
    ),
    "DVE": (
        ("XMAX", -2, 2), ("XMAX", -2, 3), ("LN3_T", -3, 0), ("FFN", -3, 0), ("XMAX", -2, 4),
        ("XMAX", -2, 5), ("XMAX", -2, 6), ("XMAX", -2, 7), ("HEADS_OUT", -1, 0),
        ("HEADS_OUT", -1, 1), ("MAX", 0, 0), ("MAX", 0, 1), ("MAX", 0, 2), ("OUT_T", -1, 0),
        ("MAX", 0, 3), ("MAX", 0, 4), ("MAX", 0, 5), ("OUT_PROJ", -1, 0), ("LN2", -1, 0),
        ("MAX", 0, 6), ("MAX", 0, 7), ("MAX", 0, 8), ("MAX", 0, 9), ("MAX", 0, 10), ("MAX", 0, 11),
        ("LN2_T", -1, 0), ("LN1", 1, 0), ("XQ", -1, 0), ("XHEADS_OUT", -2, 0),
        ("XHEADS_OUT", -2, 1), ("LN1_T", 1, 0), ("XOUT_T", -2, 0), ("K", 1, 0),
        ("XOUT_PROJ", -2, 0), ("LN3", -2, 0), ("CTX_T", 0, 0), ("Q", 1, 0), ("XMAX", -1, 0),
        ("XMAX", -1, 1), ("XK", 0, 0),
    ),
    "POOL": (
        ("LN3", -3, 0), ("FFN", -3, 0), ("LN2", -1, 0), ("LN1", 1, 0),
    ),
}
PAIRED = ("LOAD_CTX", "CTX_T", "XK", "XK_SAVE")


def step_order(engine, t):
    return [(kind, t + off, part) for kind, off, part in ORDER[engine]
            if 0 <= t + off < NSEQ and not (kind in PAIRED and t % 2)]


RINGS = {"max": 3, "score": 2, "attend": 1, "misc": 2}
FILLS = {
    "MAX": ("max", 12), "XMAX": ("max", 8),
    "SCORE": ("score", 16), "XSCORE": ("score", 8),
    "ATTEND": ("attend", 2), "XATTEND": ("attend", 2),
}
for _k in ("HEADS_OUT", "XHEADS_OUT"):
    FILLS[_k] = ("misc", 2)
for _k in ("LN1_T", "Q", "K", "V", "MAX_T", "OUT_T", "OUT_PROJ", "LN2_T", "XQ", "XMAX_T",
           "XOUT_T", "XOUT_PROJ", "LN3_T", "FFN", "CTX_T", "XK", "XV"):
    FILLS[_k] = ("misc", 1)
FIRST_STEP, LOOP_FROM, LOOP_TO, END_STEP = -2, 6, 62, NSEQ + 3


def bank_turns():
    held = {r: [None] * n for r, n in RINGS.items()}
    at = dict.fromkeys(RINGS, 0)
    turns = {}
    for t in range(FIRST_STEP, END_STEP):
        if t % 2 == 0:
            at = dict.fromkeys(RINGS, 0)
        for kind, b, part in step_order("PE", t):
            if kind not in FILLS:
                continue
            if kind in ("ATTEND", "XATTEND"):
                if part % 2:
                    continue
                part //= 2
            ring = FILLS[kind][0]
            bank = at[ring] % RINGS[ring]
            turns[kind, b, part] = bank, held[ring][bank]
            held[ring][bank] = kind, b, part
            at[ring] += 1
    for t in range(LOOP_FROM, LOOP_TO - 2):
        now = [k for k in step_order("PE", t) if k in turns]
        for kind, b, part in now:
            bank, before = turns[kind, b, part]
            later, then = turns[kind, b + 2, part]
            assert bank == later and then == (before[0], before[1] + 2, before[2])
    return turns


def build(nc, x, ctx, wts, bias, alibi, out):
    turns = bank_turns()
    with ExitStack() as stack:
        def sb(name, shape, dt=F32):
            return stack.enter_context(nc.sbuf_tensor(name, shape, dt))

        sems = {}

        def sem(name):
            if name not in sems:
                sems[name] = stack.enter_context(nc.semaphore(name))
            return sems[name]

        q_stack = [sb(f"q_stack{p}", [SHIFT + 1, H, T], F32R) for p in range(2)]
        k_stack = [sb(f"k_stack{p}", [SHIFT + 1, H, T], F32R) for p in range(2)]
        xq_stack = sb("xq_stack", [SHIFT + 1, H, T], F32R)
        xk_stack = sb("xk_stack", [SHIFT + 1, H, 2, P], F32R)
        names = ["q", "k", "v", "o", "xq", "xk", "xv", "xo", "ffn"]
        w_hi = {n: sb(f"w_{n}_hi", [P, NB, D], F32R) for n in names}
        w_lo = {n: sb(f"w_{n}_lo", [P, NB, D], F32R) for n in names}
        probs = sb("probs", [P, 8, 3 * P])
        xprobs = sb("xprobs", [P, 8, T])
        self_t = sb("self_t", [P, 2, NB, T], F32R)
        chain_t = sb("chain_t", [P, 2, NB, T], F32R)
        ctx_t = sb("ctx_t", [P, 2, NB, 2, P], F32R)
        q_nat = sb("q_nat", [P, 2, NB, T])
        k_nat = sb("k_nat", [P, 2, NB, T])
        v_aug = [sb(f"v_aug{p}", [P, NB, H * VW + HD]) for p in range(2)]
        xv_aug = [sb(f"xv_aug{p}", [C, H * VW + HD]) for p in range(2)]
        heads_t = sb("heads_t", [P, 4, T])
        self_n = sb("self_n", [P, NB, D])
        chain_n = sb("chain_n", [P, NB, D])
        x_in = [sb(f"x_in{p}", [P, NB, D]) for p in range(2)]
        res = [sb(f"res{p}", [P, NB, D]) for p in range(2)]
        ctx_in = sb("ctx_in", [C, 2, D])
        bo = {n: sb(f"bias_{n}", [P, D]) for n in ("o", "xo", "ffn")}
        bcol = {n: sb(f"bias_{n}", [P, NB]) for n in ("q", "k", "v", "xq", "xk", "xv")}
        ident = sb("ident", [P, P])
        ident_b = sb("ident_b", [P, P], BF16)
        mask_q = sb("mask_q", [P, 4, P], BF16)
        mask_k = sb("mask_k", [P, 2, P], BF16)
        neg_max = {n: sb(f"neg_max_{n}", [P, NB, H]) for n in ("s", "x")}
        neg_max_t = {n: sb(f"neg_max_t_{n}", [NB * H, P]) for n in ("s", "x")}
        rsum = sb("rsum", [P, 2, H])
        half = sb("half", [P, NB])
        ln_sb = {n: (sb(f"st_{n}", [P, NB, 6]), sb(f"mv_{n}", [P, NB, 2]), sb(f"ve_{n}", [P, NB]),
                     sb(f"rstd_{n}", [P, NB]), sb(f"mr_{n}", [P, NB]), sb(f"nmr_{n}", [P, NB]))
                 for n in ("LN1", "LN2", "LN3")}

        banks = {r: [stack.enter_context(nc.psum_tensor(f"ps_{r}{i}", [P, 512], F32))
                     for i in range(n)] for r, n in RINGS.items()}
        scr = {n: nc.dram_tensor(f"scr_{n}", [2, D, T], F32, kind="Internal").ap()
               for n in ("q", "k", "xq", "xk")}

        def seq(i, c):
            return 2 * i + c

        def wait(eng, name, per, i, c, k=0):
            if isinstance(i, int):
                b = min(2 * i + c, LAST + 1)
                v = per * b + k
                if v > 0:
                    eng.wait_ge(sem(name), v)
            else:
                assert per * c + k > 0
                eng.wait_ge(sem(name), 2 * per * i + (per * c + k))
                if eng is nc.sync:
                    alone(eng)

        def alone(eng):
            eng.sem_inc(sem("waits_carried"), 1)

        def wait_pair(eng, name, per, i, pairs):
            if isinstance(i, int):
                v = per * min(i + pairs, NSEQ // 2)
                if v > 0:
                    eng.wait_ge(sem(name), v)
            else:
                assert pairs > 0
                eng.wait_ge(sem(name), per * i + per * pairs)
                if eng is nc.sync:
                    alone(eng)

        GIVEN_BACK = {
            "MAX": ("max_taken", 12), "XMAX": ("xmax_taken", 8),
            "SCORE": ("probs_ready", 16), "XSCORE": ("xprobs_ready", 8),
            "ATTEND": ("heads_taken", 2), "XATTEND": ("xheads_taken", 2),
            "HEADS_OUT": ("heads_normed", 2), "XHEADS_OUT": ("xheads_normed", 2),
            "LN1_T": ("LN1_T_lo", 1), "LN2_T": ("LN2_T_lo", 1), "LN3_T": ("LN3_T_lo", 1),
            "Q": ("Q_lo", 1), "K": ("K_lo", 1), "V": ("v_taken", 1), "XQ": ("XQ_lo", 1),
            "OUT_T": ("OUT_T_lo", 1), "XOUT_T": ("XOUT_T_lo", 1),
            "OUT_PROJ": ("res1_done", 1), "XOUT_PROJ": ("res2_done", 1),
            "MAX_T": ("max_t_taken", 1), "XMAX_T": ("xmax_t_taken", 1),
            "FFN": ("ffn_taken", 1), "XV": ("xv_taken", 1),
            "CTX_T": ("CTX_T_lo", 1), "XK": ("XK_lo", 1),
        }

        def bank_of(kind, i, c, part=0):
            return banks[FILLS[kind][0]][turns[kind, c, part][0]]

        def take_bank(eng, kind, i, c, part=0):
            bank, before = turns[kind, c, part]
            if before is not None:
                k0, b0, p0 = before
                name, per = GIVEN_BACK[k0]
                if k0 in ("CTX_T", "XK"):
                    wait_pair(eng, name, 1, i, b0 // 2 + 1)
                else:
                    wait(eng, name, per, i, b0, p0 + 1)
            return banks[FILLS[kind][0]][bank]

        def walk(eng, name, do):
            def step(i, t):
                for kind, b, part in step_order(name, t):
                    do[kind](i, b, part)
            for t in range(FIRST_STEP, LOOP_FROM):
                step(0, t)
            with eng.Fori(0, (LOOP_TO - LOOP_FROM) // 2) as i:
                for t in range(LOOP_FROM, LOOP_FROM + 2):
                    step(i, t)
            for t in range(LOOP_TO, END_STEP):
                step(0, t)

        def blocks(tile, n=2):
            return tile[:, :].rearrange("p (a b) -> p a b", a=n)

        ws = ["q", "k", "v", "o", "xq", "xk", "xv", "xo"]
        raw_of = {}
        for n, nm in enumerate(ws[:6]):
            raw_of[nm] = probs[:, :, :].rearrange("p a b -> p (a b)")[:, n * 512:(n + 1) * 512]
        raw_of["xv"] = heads_t[:, 0:2, :].rearrange("p a b -> p (a b)")
        raw_of["xo"] = heads_t[:, 2:4, :].rearrange("p a b -> p (a b)")
        raw_of["f0"] = res[0][:, :, :].rearrange("p a b -> p (a b)")
        raw_of["f1"] = res[1][:, :, :].rearrange("p a b -> p (a b)")
        raw_of["f2"] = chain_n[:, :, :].rearrange("p a b -> p (a b)")
        raw = {n: v.rearrange("p (a b) -> p a b", a=NB) for n, v in raw_of.items()}
        xpf = xprobs[:, :, :].rearrange("p a b -> p (a b)")
        f1_t = xpf[:, 0:512].rearrange("p (a b) -> p a b", a=NB)
        f0_t = xpf[:, 512:1024].rearrange("p (a b) -> p a b", a=NB)
        f12 = xpf[:, 1024:1536].rearrange("p (a b) -> p a b", a=NB)
        PREP = ws + ["f1", "f0"]
        SCALE = {n: 1.0 for n in ws}
        SCALE["q"] = SCALE["xq"] = float(HD) ** -0.5

        block = stack.enter_context(nc.Block())

        @block.sync
        def _(sp):
            for n in PREP + ["f2"]:
                sp.dma_start(raw[n], wts[n].rearrange("(a p) c -> p a c", p=P)).then_inc(sem("w_loaded"), 16)
            for n in bcol:
                sp.dma_start(bcol[n][:, :], bias[n].rearrange("(a p) -> p a", p=P),
                             allow_slow_non_contiguous=True).then_inc(sem("b_loaded"), 16)
            for n in bo:
                sp.dma_start(bo[n][:, :], bias[n].rearrange("(a d) -> a d", a=1).broadcast_to([P, D])).then_inc(sem("b_loaded"), 16)
            for n in range(4):
                sp.dma_start(k_nat[32 * n:32 * n + 2, :, :, :].rearrange("p h a t -> p (h a t)"),
                             alibi[:, n * 4 * T:(n + 1) * 4 * T]).then_inc(sem("alibi_loaded"), 16)
            sp.wait_ge(sem("zeroed_dve"), 2)
            sp.wait_ge(sem("zeroed_pool"), 1)
            sp.wait_ge(sem("zeroed_act"), 1)
            ones = v_aug[0][0:2, 0, 0:T].unsqueeze(1).to_broadcast([2, H, T])
            for p in range(2):
                sp.dma_start(q_stack[p][AUG:AUG + 2, :, :].bitcast(F32), ones).then_inc(sem("rows_set"), 16)
                sp.dma_start(k_stack[p][SHIFT:SHIFT + 1, :, :].bitcast(F32), ones[0:1]).then_inc(sem("rows_set"), 16)
            sp.dma_start(xk_stack[SHIFT:SHIFT + 1, :, :, :].rearrange("p h s k -> p h (s k)").bitcast(F32),
                         ones[0:1]).then_inc(sem("rows_set"), 16)
            sp.wait_ge(sem("alibi_copied"), 1)
            sp.dma_start(k_stack[1][AUG:AUG + 2, :, :].bitcast(F32), k_stack[0][AUG:AUG + 2, :, :].bitcast(F32))\
                .then_inc(sem("rows_set"), 16)

            def load_x(i, b, _):
                wait(sp, "res1_done", 1, i, b - 2, 1)
                sp.dma_start(x_in[b % 2][:, :, :], x[seq(i, b)].rearrange("(a p) d -> p a d", p=P))\
                    .then_inc(sem(f"x_loaded{b % 2}"), 16)

            def load_ctx(i, b, _):
                wait_pair(sp, "CTX_T_pe", 1, i, b // 2)
                sp.dma_start(ctx_in[:, :, :], ctx[bass.ds(seq(i, b), 2)].rearrange("s c d -> c s d"))\
                    .then_inc(sem("ctx_loaded"), 16)

            def save(name, nat):
                def f(i, b, _):
                    pair = name == "xk"
                    lo = {"q": "Q_lo", "k": "K_lo", "xq": "XQ_lo", "xk": "XK_lo"}[name]
                    if pair:
                        wait_pair(sp, lo, 1, i, b // 2 + 1)
                        wait(sp, "xk_stacked", 48, i, b)
                    else:
                        wait(sp, lo, 1, i, b, 1)
                        wait(sp, f"{name}_stacked", 48, i, b)
                    sp.dma_start(scr[name].rearrange("h (a p) t -> p (h a) t", p=P),
                                 nat[:, :, :, :].rearrange("p h a t -> p (h a) t"))\
                        .then_inc(sem(f"{name}_saved"), 16)
                return f

            def restack(name):
                parts = (0, 1, 0) if name.endswith("k") else (0, 0, 1)

                def f(i, b, _):
                    if name == "xk":
                        wait_pair(sp, "xk_saved", 16, i, b // 2 + 1)
                        wait(sp, "xscores_ready", 8, i, b - 1)
                    elif name == "xq":
                        wait(sp, "xq_saved", 16, i, b + 1)
                        wait(sp, "xscores_ready", 8, i, b)
                    else:
                        wait(sp, f"{name}_saved", 16, i, b + 1)
                        wait(sp, "scores_ready", 16, i, b - 1)
                    for n, half_ in enumerate(parts):
                        rows = scr[name][half_].rearrange("(h d) t -> d h t", d=HD)
                        if name == "xk":
                            dst = xk_stack[n * HD:(n + 1) * HD, :, b % 2, :]
                            rows = rows[:, :, (b % 2) * P:(b % 2 + 1) * P]
                        else:
                            dst = {"q": q_stack, "k": k_stack, "xq": [xq_stack] * 2}[name][b % 2][
                                n * HD:(n + 1) * HD, :, :]
                        sp.dma_start(dst.bitcast(F32), rows).then_inc(sem(f"{name}_stacked"), 16)
                return f

            def stack_max(which, dst_of):
                def f(i, b, _):
                    wait(sp, {"s": "max_t_taken", "x": "xmax_t_taken"}[which], 1, i, b, 1)
                    for qb in range(NB):
                        sp.dma_start(dst_of(b)[SHIFT:SHIFT + 1, :, qb * P:(qb + 1) * P].bitcast(F32),
                                     neg_max_t[which][qb * H:(qb + 1) * H, :])\
                            .then_inc(sem(f"{which}_shift_stacked"), 16)
                return f

            def store(i, b, _):
                wait(sp, "out_ready", 1, i, b, 1)
                sp.dma_start(out[seq(i, b)].rearrange("(a p) d -> p a d", p=P), res[b % 2][:, :, :])\
                    .then_inc(sem(f"stored{b % 2}"), 16)

            walk(sp, "SP", {
                "LOAD_X": load_x, "LOAD_CTX": load_ctx,
                "Q_SAVE": save("q", q_nat), "K_SAVE": save("k", k_nat),
                "XQ_SAVE": save("xq", q_nat), "XK_SAVE": save("xk", k_nat),
                "Q_STACK": restack("q"), "K_STACK": restack("k"),
                "XQ_STACK": restack("xq"), "XK_STACK": restack("xk"),
                "MAX_STACK": stack_max("s", lambda b: q_stack[b % 2]),
                "XMAX_STACK": stack_max("x", lambda b: xq_stack),
                "STORE": store,
            })
            for p in range(2):
                sp.wait_ge(sem(f"stored{p}"), 16 * NSEQ // 2)

        @block.tensor
        def _(pe):
            pe.wait_ge(sem("consts"), 4)
            pe.wait_ge(sem("w_loaded"), 16 * (len(PREP) + 1))
            for n, nm in enumerate(PREP):
                if n >= 2:
                    pe.wait_ge(sem("prep_lo"), n - 1)
                bk = blocks(banks["misc"][n % 2])
                for a in range(NB):
                    for k in range(NB):
                        mm = pe.transpose(bk[:, k, a * P:(a + 1) * P], raw[nm][:, a, k * P:(k + 1) * P],
                                          ident[:, :])
                mm.then_inc(sem("pe_prep"), 1)
            for stage, (lhs, rhs) in enumerate(((f1_t, raw["f2"]), (f0_t, f12))):
                pe.wait_ge(sem("prep_lo"), len(PREP) + stage)
                bk = blocks(banks["misc"][stage])
                for m in range(NB):
                    for k in range(NB):
                        mm = pe.matmul(bk[:, m, :], lhs[:, k, m * P:(m + 1) * P], rhs[:, k, :],
                                       start=(k == 0), stop=(k == NB - 1))
                mm.then_inc(sem("pe_prep"), 1)
            pe.wait_ge(sem("prep_lo"), len(PREP) + 2)

            def transposes(kind, src, ready, last):
                def f(i, b, _):
                    wait(pe, ready, 1, i, b, 1)
                    bk = blocks(take_bank(pe, kind, i, b))
                    for a in range(NB):
                        for k in range(NB):
                            mm = pe.transpose(bk[:, k, a * P:(a + 1) * P],
                                              src[:, a, k * P:(k + 1) * P], ident[:, :])
                    mm.then_inc(sem(f"{kind}_pe"), 1)
                return f

            def dims_out(kind, w, src_t, ready, pair=False):
                def f(i, b, _):
                    if pair:
                        wait_pair(pe, ready, 1, i, b // 2 + 1)
                    else:
                        wait(pe, ready, 1, i, b, 1)
                    bk = blocks(take_bank(pe, kind, i, b))
                    for m in range(NB):
                        for k in range(NB):
                            for n, (wt, h) in enumerate(((w_hi, 0), (w_hi, 1), (w_lo, 0))):
                                mm = pe.matmul(bk[:, m, :], wt[w][:, k, m * P:(m + 1) * P],
                                               src_t(h, k), start=(k == 0 and n == 0),
                                               stop=(k == NB - 1 and n == 2))
                    mm.then_inc(sem(f"{kind}_pe"), 1)
                return f

            def tokens_out(kind, w, src_t, ready):
                def f(i, b, _):
                    wait(pe, ready, 1, i, b, 1)
                    bk = blocks(take_bank(pe, kind, i, b))
                    for m in range(NB):
                        for k in range(NB):
                            for n, (h, wt) in enumerate(((0, w_hi), (0, w_lo), (1, w_hi))):
                                mm = pe.matmul(bk[:, m, :], src_t(h, k)[:, m * P:(m + 1) * P],
                                               wt[w][:, k, :], start=(k == 0 and n == 0),
                                               stop=(k == NB - 1 and n == 2))
                    mm.then_inc(sem(f"{kind}_pe"), 1)
                return f

            def context_values(i, b, _):
                wait_pair(pe, "CTX_T_lo", 1, i, b // 2 + 1)
                bk = take_bank(pe, "XV", i, b)
                for k in range(NB):
                    for n, (h, wt) in enumerate(((0, w_hi), (0, w_lo), (1, w_hi))):
                        mm = pe.matmul(bk[0:C, 0:D], ctx_t[:, h, k, b % 2, 0:C], wt["xv"][:, k, :],
                                       start=(k == 0 and n == 0), stop=(k == NB - 1 and n == 2))
                mm.then_inc(sem("XV_pe"), 1)

            def context_transposes(i, b, _):
                wait_pair(pe, "ctx_loaded", 16, i, b // 2 + 1)
                bk = take_bank(pe, "CTX_T", i, b)[:, :].rearrange("p (k s c) -> p k s c", k=NB, s=2)
                for s in range(2):
                    for k in range(NB):
                        mm = pe.transpose(bk[:, k, s, 0:C], ctx_in[:, s, k * P:(k + 1) * P],
                                          ident[0:C, 0:C])
                mm.then_inc(sem("CTX_T_pe"), 1)

            def narrow(ap):
                return ap.bitcast(BF16)[:, 1::2]

            def maxima(i, b, u):
                if u == 0:
                    if isinstance(i, int) and b == 0:
                        pe.wait_ge(sem("rows_set"), 16 * 6)
                    wait(pe, "q_stacked", 48, i, b, 48)
                    wait(pe, "k_stacked", 48, i, b, 48)
                bk = take_bank(pe, "MAX", i, b, u)
                qs, ks = q_stack[b % 2], k_stack[b % 2]
                g, what = u // 3, u % 3
                if what == 0:
                    pe.matmul(bk[:, :], ident_b[:, :], mask_q[:, :, :].rearrange("p a b -> p (a b)"),
                              start=True, stop=False, skip_group_check=True)
                    for j in range(4):
                        mm = pe.matmul(bk[:, j * P:(j + 1) * P], narrow(qs[0:SHIFT, 4 * g + j, 0:P]),
                                       narrow(ks[0:SHIFT, 4 * g + j, 0:P]), start=False, stop=(j == 3),
                                       skip_group_check=True)
                else:
                    two = blocks(bk)
                    pe.matmul(two[:, :, P:T], ident_b[:, :], mask_q[:, 0:2, :],
                              start=True, stop=False, skip_group_check=True)
                    for j in range(2):
                        h = 4 * g + 2 * (what - 1) + j
                        mm = pe.matmul(two[:, j, :], narrow(qs[0:SHIFT, h, P:T]),
                                       narrow(ks[0:SHIFT, h, :]), start=False, stop=(j == 1),
                                       skip_group_check=True)
                mm.then_inc(sem("max_ready"), 1)

            def cross_maxima(i, b, u):
                if u == 0:
                    wait(pe, "xq_stacked", 48, i, b, 48)
                    wait(pe, "xk_stacked", 48, i, b, 48)
                bk = take_bank(pe, "XMAX", i, b, u)
                g, qb = u // 2, u % 2
                for j in range(4):
                    h = 4 * g + j
                    mm = pe.matmul(bk[:, j * C:(j + 1) * C], narrow(xq_stack[0:SHIFT, h, qb * P:(qb + 1) * P]),
                                   narrow(xk_stack[0:SHIFT, h, b % 2, 0:C]), start=True, stop=True)
                mm.then_inc(sem("xmax_ready"), 1)

            def max_transpose(kind, which, taken, per):
                def f(i, b, _):
                    wait(pe, taken, per, i, b, per)
                    bk = take_bank(pe, kind, i, b)
                    pe.transpose(bk[0:NB * H, 0:P], neg_max[which][:, :, :].rearrange("p a h -> p (a h)"),
                                 ident[:, :]).then_inc(sem(f"{kind}_pe"), 1)
                return f

            def scores(i, b, h):
                if h == 0:
                    wait(pe, "s_shift_stacked", 32, i, b, 32)
                bk = take_bank(pe, "SCORE", i, b, h)
                qs, ks = q_stack[b % 2], k_stack[b % 2]
                pe.matmul(bk[:, P:3 * P], ident_b[:, :], mask_k[:, :, :].rearrange("p a b -> p (a b)"),
                          start=True, stop=False, skip_group_check=True)
                pe.matmul(bk[:, 0:T], ks[:, h, P:T], qs[:, h, :], start=False, stop=False,
                          skip_group_check=True)
                pe.matmul(bk[:, T:2 * T], ks[:, h, 0:P], qs[:, h, :], start=False, stop=True,
                          skip_group_check=True).then_inc(sem("scores_ready"), 1)

            def cross_scores(i, b, u):
                if u == 0:
                    wait(pe, "x_shift_stacked", 32, i, b, 32)
                bk = take_bank(pe, "XSCORE", i, b, u)
                for j in range(2):
                    h = 2 * u + j
                    mm = pe.matmul(bk[0:C, j * T:(j + 1) * T], xk_stack[:, h, b % 2, 0:C],
                                   xq_stack[:, h, :], start=True, stop=True)
                mm.then_inc(sem("xscores_ready"), 1)

            def attend(i, b, g):
                if g == 0:
                    wait(pe, "v_taken", 1, i, b, 1)
                if g % 2 == 0:
                    take_bank(pe, "ATTEND", i, b, g // 2)
                bk = banks["attend"][0]
                wait(pe, "probs_ready", 16, i, b, 4 * g + 4)
                at = (g % 2) * T
                for j in range(4):
                    h = 4 * g + j
                    pe.matmul(bk[32 * j:32 * j + 32, at:at + T], v_aug[b % 2][:, 0, h * VW:h * VW + 32],
                              probs[:, h % 8, P:3 * P], start=True, stop=False, skip_group_check=True)
                for j in range(4):
                    h = 4 * g + j
                    mm = pe.matmul(bk[32 * j:32 * j + 32, at + P:at + T],
                                   v_aug[b % 2][:, 1, h * VW:h * VW + 32], probs[:, h % 8, 0:P],
                                   start=False, stop=True, skip_group_check=True)
                mm.then_inc(sem("attended"), 1)

            def cross_attend(i, b, g):
                if g == 0:
                    wait(pe, "xv_taken", 1, i, b, 1)
                if g % 2 == 0:
                    take_bank(pe, "XATTEND", i, b, g // 2)
                bk = banks["attend"][0]
                wait(pe, "xprobs_ready", 8, i, b, 2 * g + 2)
                at = (g % 2) * T
                for j in range(4):
                    h = 4 * g + j
                    mm = pe.matmul(bk[32 * j:32 * j + 32, at:at + T], xv_aug[b % 2][:, h * VW:h * VW + 32],
                                   xprobs[0:C, h % 8, :], start=True, stop=True, skip_group_check=True)
                mm.then_inc(sem("xattended"), 1)

            def heads_out(kind, taken):
                def f(i, b, qb):
                    if qb == 0:
                        wait(pe, taken, 2, i, b, 2)
                    bk = take_bank(pe, kind, i, b, qb)
                    for g in range(4):
                        mm = pe.transpose(bk[:, g * P:(g + 1) * P], heads_t[:, g, qb * P:(qb + 1) * P],
                                          ident[:, :])
                    mm.then_inc(sem(f"{kind}_pe"), 1)
                return f

            self_of = lambda h, k: self_t[:, h, k, :]
            chain_of = lambda h, k: chain_t[:, h, k, :]
            ctx_of = lambda h, k: ctx_t[:, h, k, :, :].rearrange("p s c -> p (s c)")

            def norm_transposes(kind, normed):
                def f(i, b, _):
                    wait(pe, normed, 2, i, b, 2)
                    bk = blocks(take_bank(pe, kind, i, b))
                    for a in range(NB):
                        for k in range(NB):
                            mm = pe.transpose(bk[:, k, a * P:(a + 1) * P],
                                              chain_n[:, a, k * P:(k + 1) * P], ident[:, :])
                    mm.then_inc(sem(f"{kind}_pe"), 1)
                return f

            walk(pe, "PE", {
                "LN1_T": transposes("LN1_T", self_n, "LN1_done", None),
                "LN2_T": transposes("LN2_T", chain_n, "LN2_done", None),
                "LN3_T": transposes("LN3_T", chain_n, "LN3_done", None),
                "OUT_T": norm_transposes("OUT_T", "heads_normed"),
                "XOUT_T": norm_transposes("XOUT_T", "xheads_normed"),
                "Q": dims_out("Q", "q", self_of, "LN1_T_lo"),
                "K": dims_out("K", "k", self_of, "LN1_T_lo"),
                "V": tokens_out("V", "v", self_of, "LN1_T_lo"),
                "XQ": dims_out("XQ", "xq", chain_of, "LN2_T_lo"),
                "XK": dims_out("XK", "xk", ctx_of, "CTX_T_lo", pair=True),
                "XV": context_values,
                "CTX_T": context_transposes,
                "OUT_PROJ": tokens_out("OUT_PROJ", "o", chain_of, "OUT_T_lo"),
                "XOUT_PROJ": tokens_out("XOUT_PROJ", "xo", chain_of, "XOUT_T_lo"),
                "FFN": tokens_out("FFN", "ffn", chain_of, "LN3_T_lo"),
                "MAX": maxima, "XMAX": cross_maxima,
                "MAX_T": max_transpose("MAX_T", "s", "max_taken", 12),
                "XMAX_T": max_transpose("XMAX_T", "x", "xmax_taken", 8),
                "SCORE": scores, "XSCORE": cross_scores,
                "ATTEND": attend, "XATTEND": cross_attend,
                "HEADS_OUT": heads_out("HEADS_OUT", "heads_taken"),
                "XHEADS_OUT": heads_out("XHEADS_OUT", "xheads_taken"),
            })

        SPLITS = {
            "LN1_T": (None, self_t), "LN2_T": (None, chain_t), "LN3_T": (None, chain_t),
            "OUT_T": ("v", chain_t), "XOUT_T": ("xv", chain_t),
            "Q": ("q", q_nat), "K": ("k", k_nat), "XQ": ("xq", q_nat), "XK": ("xk", k_nat),
            "CTX_T": (None, ctx_t),
        }

        @block.scalar
        def _(act):
            act.wait_ge(sem("consts"), 4)
            act.activation(ctx_t[:, :, :, :, :].rearrange("p h a s c -> p (h a s c)"),
                           ident[:, 0:1].to_broadcast([P, 4 * T]), ACT.Copy, scale=0.0)
            act.activation(xq_stack[:, :, :].rearrange("p h t -> p (h t)"),
                           ident[0:SHIFT + 1, 0:1].to_broadcast([SHIFT + 1, H * T]), ACT.Copy,
                           scale=0.0).then_inc(sem("zeroed_act"), 1)
            for n, nm in enumerate(PREP):
                act.wait_ge(sem("pe_prep"), n + 1)
                bk = blocks(banks["misc"][n % 2])
                if nm in SCALE:
                    act.activation(w_hi[nm][:, :, :], bk, ACT.Copy, scale=SCALE[nm]).then_inc(sem("prep_hi"), 1)
                else:
                    act.activation({"f1": f1_t, "f0": f0_t}[nm], bk, ACT.Copy).then_inc(sem("prep_hi"), 1)
            act.wait_ge(sem("pe_prep"), len(PREP) + 1)
            act.activation(f12, blocks(banks["misc"][0]), ACT.Copy).then_inc(sem("prep_hi"), 1)
            act.wait_ge(sem("pe_prep"), len(PREP) + 2)
            act.activation(w_hi["ffn"][:, :, :], blocks(banks["misc"][1]), ACT.Copy).then_inc(sem("prep_hi"), 1)
            act.wait_ge(sem("b_loaded"), 16 * 9)
            act.wait_ge(sem("b_scaled"), 1)

            def hi(kind, free):
                bias_of, dst = SPLITS[kind]

                def f(i, b, _):
                    if kind in ("CTX_T", "XK"):
                        wait_pair(act, f"{kind}_pe", 1, i, b // 2 + 1)
                    else:
                        wait(act, f"{kind}_pe", 1, i, b, 1)
                    free(i, b)
                    bk = blocks(bank_of(kind, i, b))
                    if kind == "CTX_T":
                        act.activation(dst[:, 0, :, :, 0:C].rearrange("p a s c -> p (a s) c"),
                                       bank_of(kind, i, b)[:, :].rearrange("p (a c) -> p a c", a=4)[:, :, 0:C],
                                       ACT.Copy).then_inc(sem(f"{kind}_hi"), 1)
                    elif bias_of is None:
                        act.activation(dst[:, 0, :, :], bk, ACT.Copy).then_inc(sem(f"{kind}_hi"), 1)
                    else:
                        for k in range(NB):
                            o = dst[:, 0, k, :]
                            if dst is q_nat or dst is k_nat:
                                o = o.bitcast(F32R)
                            last = act.activation(o, bk[:, k, :], ACT.Identity, bias=bcol[bias_of][:, k:k + 1])
                        last.then_inc(sem(f"{kind}_hi"), 1)
                return f

            def exp_self(i, b, h):
                wait(act, "scores_ready", 16, i, b, h + 1)
                wait(act, "attended", 4, i, b, h // 4 - 1)
                act.activation(probs[:, h % 8, :], bank_of("SCORE", i, b, h)[:, P:4 * P], ACT.Exp)\
                    .then_inc(sem("probs_ready"), 1)

            def exp_cross(i, b, u):
                wait(act, "xscores_ready", 8, i, b, u + 1)
                wait(act, "xattended", 4, i, b, u // 2 - 1)
                at = 2 * u % 8
                act.activation(xprobs[0:C, at:at + 2, :], blocks(bank_of("XSCORE", i, b, u))[0:C],
                               ACT.Exp).then_inc(sem("xprobs_ready"), 1)

            def take_heads(kind, ready, other, ahead):
                def f(i, b, g):
                    if g % 2 == 0:
                        return
                    wait(act, ready, 4, i, b, g + 1)
                    if g == 1:
                        wait(act, other, 2, i, b + ahead, 0)
                    act.activation(heads_t[:, g - 1:g + 1, :], blocks(banks["attend"][0]), ACT.Copy)\
                        .then_inc(sem({"ATTEND": "heads_taken", "XATTEND": "xheads_taken"}[kind]), 1)
                return f

            def take_v(i, b, _):
                wait(act, "V_pe", 1, i, b, 1)
                wait(act, "attended", 4, i, b - 1)
                act.activation(v_aug[b % 2][:, :, 0:H * VW].rearrange("p a (h w) -> p a h w", w=VW)[:, :, :, 0:HD],
                               bank_of("V", i, b)[:, :].rearrange("p (a h w) -> p a h w", a=NB, w=HD),
                               ACT.Copy).then_inc(sem("v_taken"), 1)

            def take_xv(i, b, _):
                wait(act, "XV_pe", 1, i, b, 1)
                wait(act, "xattended", 4, i, b - 1)
                act.activation(xv_aug[b % 2][:, 0:H * VW].rearrange("p (h w) -> p h w", w=VW)[:, :, 0:HD],
                               bank_of("XV", i, b)[0:C, 0:D].rearrange("p (h w) -> p h w", w=HD),
                               ACT.Copy).then_inc(sem("xv_taken"), 1)

            def take_max_t(kind, which, stacked, taken):
                def f(i, b, _):
                    wait(act, f"{kind}_pe", 1, i, b, 1)
                    wait(act, stacked, 32, i, b)
                    act.activation(neg_max_t[which][:, :].bitcast(F32R), bank_of(kind, i, b)[0:NB * H, 0:P],
                                   ACT.Copy).then_inc(sem(taken), 1)
                return f

            def tanh(i, b, _):
                wait(act, "ffn_taken", 1, i, b, 1)
                act.activation(chain_n[:, :, :], chain_n[:, :, :], ACT.Tanh).then_inc(sem("tanh_done"), 1)

            def k_free(i, b):
                wait_pair(act, "xk_saved", 16, i, b // 2)

            walk(act, "ACT", {
                "LN1_T": hi("LN1_T", lambda i, b: wait(act, "V_pe", 1, i, b)),
                "LN2_T": hi("LN2_T", lambda i, b: None),
                "LN3_T": hi("LN3_T", lambda i, b: None),
                "OUT_T": hi("OUT_T", lambda i, b: wait(act, "FFN_pe", 1, i, b - 1)),
                "XOUT_T": hi("XOUT_T", lambda i, b: wait(act, "XQ_pe", 1, i, b + 2)),
                "CTX_T": hi("CTX_T", lambda i, b: wait(act, "XV_pe", 1, i, b)),
                "Q": hi("Q", lambda i, b: wait(act, "xq_saved", 16, i, b - 1)),
                "XQ": hi("XQ", lambda i, b: wait(act, "q_saved", 16, i, b + 2)),
                "K": hi("K", k_free),
                "XK": hi("XK", lambda i, b: wait(act, "k_saved", 16, i, b + 2)),
                "V": take_v, "XV": take_xv,
                "SCORE": exp_self, "XSCORE": exp_cross,
                "ATTEND": take_heads("ATTEND", "attended", "XHEADS_OUT_pe", -1),
                "XATTEND": take_heads("XATTEND", "xattended", "HEADS_OUT_pe", 2),
                "MAX_T": take_max_t("MAX_T", "s", "s_shift_stacked", "max_t_taken"),
                "XMAX_T": take_max_t("XMAX_T", "x", "x_shift_stacked", "xmax_t_taken"),
                "FFN": tanh,
            })

        @block.vector
        def _(dve):
            dve.memset(half[:, :], -0.5)
            for p in range(2):
                dve.memset(v_aug[p][:, :, :], 1.0)
                dve.memset(xv_aug[p][:, :], 1.0)
            dve.memset(k_stack[0][:, :, :].bitcast(F32), 0.0).then_inc(sem("zeroed_dve"), 1)
            dve.wait_ge(sem("zeroed_dve"), 1)
            dve.wait_ge(sem("alibi_loaded"), 16 * 4)
            for n in range(4):
                last = dve.tensor_copy(k_stack[0][AUG:AUG + 2, 4 * n:4 * n + 4, :].rearrange("p h t -> p (h t)"),
                                       k_nat[32 * n:32 * n + 2, :, :, :].rearrange("p h a t -> p (h a t)"))
            last.then_inc(sem("alibi_copied"), 1)
            dve.memset(q_stack[0][:, :, :].bitcast(F32), 0.0).then_inc(sem("zeroed_dve"), 1)
            dve.wait_ge(sem("b_loaded"), 16 * 9)
            dve.tensor_scalar(bcol["q"][:, :], bcol["q"][:, :], SCALE["q"], None, ALU.mult)
            dve.tensor_scalar(bcol["xq"][:, :], bcol["xq"][:, :], SCALE["xq"], None, ALU.mult)\
                .then_inc(sem("b_scaled"), 1)
            for n, nm in enumerate(PREP + ["f12", "ffn"]):
                dve.wait_ge(sem("prep_hi"), n + 1)
                if nm in SCALE or nm == "ffn":
                    bk = blocks(banks["misc"][n % 2])
                    dve.scalar_tensor_tensor(out=w_lo[nm][:, :, :], in0=bk, scalar=SCALE.get(nm, 1.0),
                                             in1=w_hi[nm][:, :, :].bitcast(F32), op0=ALU.mult,
                                             op1=ALU.subtract).then_inc(sem("prep_lo"), 1)
                else:
                    dve.engine_nop().then_inc(sem("prep_lo"), 1)

            def lo(kind):
                bias_of, dst = SPLITS[kind]

                def f(i, b, _):
                    if kind in ("CTX_T", "XK"):
                        wait_pair(dve, f"{kind}_hi", 1, i, b // 2 + 1)
                    else:
                        wait(dve, f"{kind}_hi", 1, i, b, 1)
                    bk = blocks(bank_of(kind, i, b))
                    if kind == "CTX_T":
                        v = lambda h: dst[:, h, :, :, 0:C].rearrange("p a s c -> p (a s) c")
                        last = dve.tensor_tensor(
                            v(1), bank_of(kind, i, b)[:, :].rearrange("p (a c) -> p a c", a=4)[:, :, 0:C],
                            v(0).bitcast(F32), ALU.subtract)
                    elif bias_of is None:
                        last = dve.tensor_tensor(dst[:, 1, :, :], bk, dst[:, 0, :, :].bitcast(F32), ALU.subtract)
                    else:
                        for k in range(NB):
                            o = dst[:, 1, k, :]
                            if dst is q_nat or dst is k_nat:
                                o = o.bitcast(F32R)
                            last = dve.scalar_tensor_tensor(
                                out=o, in0=bk[:, k, :], scalar=bcol[bias_of][:, k:k + 1],
                                in1=dst[:, 0, k, :].bitcast(F32), op0=ALU.add, op1=ALU.subtract)
                    last.then_inc(sem(f"{kind}_lo"), 1)
                return f

            def maxima(i, b, u):
                wait(dve, "max_ready", 12, i, b, u + 1)
                if u == 0:
                    wait(dve, "MAX_T_pe", 1, i, b)
                g, what = u // 3, u % 3
                bk = bank_of("MAX", i, b, u)
                if what == 0:
                    ins, o = blocks(bk, 4), neg_max["s"][:, 0, 4 * g:4 * g + 4]
                else:
                    h = 4 * g + 2 * (what - 1)
                    ins, o = blocks(bk), neg_max["s"][:, 1, h:h + 2]
                dve.tensor_reduce(o, ins, AX.X, ALU.max, negate=True).then_inc(sem("max_taken"), 1)

            def cross_maxima(i, b, u):
                wait(dve, "xmax_ready", 8, i, b, u + 1)
                if u == 0:
                    wait(dve, "XMAX_T_pe", 1, i, b)
                g, qb = u // 2, u % 2
                bk = bank_of("XMAX", i, b, u)[:, 0:4 * C].rearrange("p (a c) -> p a c", a=4)
                dve.tensor_reduce(neg_max["x"][:, qb, 4 * g:4 * g + 4], bk, AX.X, ALU.max,
                                  negate=True).then_inc(sem("xmax_taken"), 1)

            def moments(kind, src, ready):
                st, mv = ln_sb[kind][0:2]

                def f(i, b, _):
                    ready(i, b)
                    wait(dve, f"{kind}_done", 1, i, b)
                    for a in range(NB):
                        dve.bn_stats(st[:, a, :], src[b % 2][:, a, :]).then_inc(sem(f"{kind}_stats"), 1)
                    wait(dve, f"{kind}_stats", 2, i, b, 2)
                    alone(dve)
                    for a in range(NB):
                        last = dve.bn_aggr(mv[:, a, :], st[:, a, :])
                    last.then_inc(sem(f"{kind}_moments"), 1)
                return f

            def x_ready(i, b):
                wait_x(dve, i, b)

            def wait_x(eng, i, b):
                v = 16 * (b // 2 + 1)
                eng.wait_ge(sem(f"x_loaded{b % 2}"), v if isinstance(i, int) else 16 * i + v)

            def norm_heads(kind, done, free):
                def f(i, b, qb):
                    wait(dve, f"{kind}_pe", 2, i, b, qb + 1)
                    if qb == 0:
                        free(i, b)
                    bk = bank_of(kind, i, b, qb)[:, :].rearrange("p (h w) -> p h w", w=32)
                    rs = rsum[:, qb, :]
                    dve.reciprocal(rs.unsqueeze(2), bk[:, :, HD:HD + 1]).then_inc(sem(f"{kind}_rsum"), 1)
                    wait(dve, f"{kind}_rsum", 2, i, b, qb + 1)
                    dve.tensor_tensor(chain_n[:, qb, :].rearrange("p (h w) -> p h w", w=HD),
                                      bk[:, :, 0:HD], rs.unsqueeze(2).to_broadcast([P, H, HD]),
                                      ALU.mult).then_inc(sem(done), 1)
                return f

            def residual1(i, b, _):
                wait(dve, "OUT_PROJ_pe", 1, i, b, 1)
                wait(dve, "x_biased", 1, i, b, 1)
                v = 16 * (b // 2)
                if not isinstance(i, int) or v > 0:
                    dve.wait_ge(sem(f"stored{b % 2}"), v if isinstance(i, int) else 16 * i + v)
                dve.tensor_tensor(res[b % 2][:, :, :], blocks(bank_of("OUT_PROJ", i, b)),
                                  x_in[b % 2][:, :, :], ALU.add).then_inc(sem("res1_done"), 1)

            def residual2(i, b, _):
                wait(dve, "XOUT_PROJ_pe", 1, i, b, 1)
                wait(dve, "res_biased", 1, i, b, 1)
                dve.tensor_tensor(res[b % 2][:, :, :], blocks(bank_of("XOUT_PROJ", i, b)),
                                  res[b % 2][:, :, :], ALU.add).then_inc(sem("res2_done"), 1)

            def ffn_bias(i, b, _):
                wait(dve, "FFN_pe", 1, i, b, 1)
                bk = blocks(bank_of("FFN", i, b))
                dve.tensor_tensor(chain_n[:, :, :], bk,
                                  bo["ffn"][:, :].unsqueeze(1).to_broadcast([P, NB, D]), ALU.add)\
                    .then_inc(sem("ffn_taken"), 1)

            do = {k: lo(k) for k in SPLITS}
            do.update({
                "MAX": maxima, "XMAX": cross_maxima,
                "LN1": moments("LN1", x_in, x_ready),
                "LN2": moments("LN2", res, lambda i, b: wait(dve, "res1_done", 1, i, b, 1)),
                "LN3": moments("LN3", res, lambda i, b: wait(dve, "res2_done", 1, i, b, 1)),
                "HEADS_OUT": norm_heads("HEADS_OUT", "heads_normed",
                                        lambda i, b: wait(dve, "out_ready", 1, i, b - 1)),
                "XHEADS_OUT": norm_heads("XHEADS_OUT", "xheads_normed",
                                         lambda i, b: wait(dve, "LN2_T_pe", 1, i, b + 2)),
                "OUT_PROJ": residual1, "XOUT_PROJ": residual2, "FFN": ffn_bias,
            })
            walk(dve, "DVE", do)

        @block.gpsimd
        def _(pool):
            pool.memset(ident[:, :], 0.0).then_inc(sem("const0"), 1)
            pool.memset(ident_b[:, :], 0.0).then_inc(sem("const0"), 1)
            pool.memset(mask_q[:, :, :], 0.0).then_inc(sem("const0"), 1)
            pool.memset(mask_k[:, :, :], 0.0).then_inc(sem("const0"), 1)
            pool.wait_ge(sem("const0"), 4)
            for m in (ident, ident_b):
                pool.affine_select(out=m[:, :], in_=m[:, :], compare_op=ALU.not_equal, fill=1.0, base=0,
                                   pattern=[[-1, P]], channel_multiplier=1).then_inc(sem("consts"), 1)
            pool.affine_select(out=mask_q[:, :, :], in_=mask_q[:, :, :], compare_op=ALU.is_ge, fill=BIG,
                               base=0, pattern=[[0, 4], [-1, P]], channel_multiplier=1)\
                .then_inc(sem("consts"), 1)
            pool.affine_select(out=mask_k[:, :, :], in_=mask_k[:, :, :], compare_op=ALU.is_ge, fill=BIG,
                               base=0, pattern=[[0, 2], [1, P]], channel_multiplier=-1)\
                .then_inc(sem("consts"), 1)
            pool.memset(k_stack[1][:, :, :].bitcast(F32), 0.0)
            pool.memset(q_stack[1][:, :, :].bitcast(F32), 0.0)
            pool.memset(xk_stack[:, :, :, :].bitcast(F32), 0.0).then_inc(sem("zeroed_pool"), 1)
            pool.wait_ge(sem("b_loaded"), 16 * 9)
            pool.wait_ge(sem("zeroed_dve"), 1)

            def normalise(kind, src, dst, free, bias_name, biased):
                st, mv, ve, rstd, mr, nmr = ln_sb[kind]

                def f(i, b, _):
                    wait(pool, f"{kind}_moments", 1, i, b, 1)
                    alone(pool)
                    s = f"{kind}_small"
                    pool.tensor_scalar(ve[:, :].unsqueeze(2), mv[:, :, 1:2], 1.0, EPS, ALU.mult, ALU.add)\
                        .then_inc(sem(s), 1)
                    wait(pool, s, 4, i, b, 1)
                    pool.tensor_tensor(rstd[:, :], ve[:, :], half[:, :], ALU.pow).then_inc(sem(s), 1)
                    wait(pool, s, 4, i, b, 2)
                    pool.tensor_tensor(mr[:, :].unsqueeze(2), mv[:, :, 0:1], rstd[:, :].unsqueeze(2), ALU.mult)\
                        .then_inc(sem(s), 1)
                    wait(pool, s, 4, i, b, 3)
                    alone(pool)
                    pool.tensor_scalar(nmr[:, :], mr[:, :], -1.0, 0.0, ALU.mult, ALU.add).then_inc(sem(s), 1)
                    wait(pool, s, 4, i, b, 4)
                    free(i, b)
                    alone(pool)
                    for a in range(NB):
                        last = pool.tensor_scalar(dst[:, a, :], src[b % 2][:, a, :], rstd[:, a:a + 1],
                                                  nmr[:, a:a + 1], ALU.mult, ALU.add)
                    last.then_inc(sem(f"{kind}_done"), 1)
                    if bias_name:
                        wait(pool, f"{kind}_done", 1, i, b, 1)
                        pool.tensor_tensor(src[b % 2][:, :, :], src[b % 2][:, :, :],
                                           bo[bias_name][:, :].unsqueeze(1).to_broadcast([P, NB, D]),
                                           ALU.add).then_inc(sem(biased), 1)
                return f

            def finish(i, b, _):
                wait(pool, "tanh_done", 1, i, b, 1)
                pool.tensor_tensor(res[b % 2][:, :, :], res[b % 2][:, :, :], chain_n[:, :, :], ALU.add)\
                    .then_inc(sem("out_ready"), 1)

            walk(pool, "POOL", {
                "LN1": normalise("LN1", x_in, self_n, lambda i, b: wait(pool, "LN1_T_pe", 1, i, b),
                                 "o", "x_biased"),
                "LN2": normalise("LN2", res, chain_n, lambda i, b: None, "xo", "res_biased"),
                "LN3": normalise("LN3", res, chain_n, lambda i, b: None, None, None),
                "FFN": finish,
            })



def alibi_rows():
    def upper(v):
        top = np.exp2(np.floor(np.log2(np.maximum(np.abs(v), 1e-30))))
        return np.round(v / top * 2048) / 2048 * top


    slopes = (2.0 ** (-8.0 * np.arange(1, H + 1, dtype=np.float64) / H)).astype(np.float32)
    v = slopes.astype(np.float64)[:, None] * (np.arange(T, dtype=np.float64) - T // 2)[None, :]
    hi = upper(v)
    return np.stack([hi, upper(v - hi)]).astype(np.float32).reshape(2, H * T)



def kernel(x, ctx_1024, L0_attn_Wq, L0_attn_bq, L0_attn_Wk, L0_attn_bk, L0_attn_Wv, L0_attn_bv,
           L0_attn_Wo, L0_attn_bo, L0_xattn_Wq, L0_xattn_bq, L0_xattn_Wk, L0_xattn_bk, L0_xattn_Wv,
           L0_xattn_bv, L0_xattn_Wo, L0_xattn_bo, L0_ffn_weight, L0_ffn_aux_weight1,
           L0_ffn_aux_weight2, L0_ffn_bias):
    import concourse.bacc as bacc
    from concourse.bass_utils import run_bass_kernel_spmd

    given = {
        "x": x, "ctx": ctx_1024, "w_q": L0_attn_Wq, "w_k": L0_attn_Wk, "w_v": L0_attn_Wv,
        "w_o": L0_attn_Wo, "w_xq": L0_xattn_Wq, "w_xk": L0_xattn_Wk, "w_xv": L0_xattn_Wv,
        "w_xo": L0_xattn_Wo, "w_f0": L0_ffn_weight, "w_f1": L0_ffn_aux_weight1,
        "w_f2": L0_ffn_aux_weight2, "b_q": L0_attn_bq, "b_k": L0_attn_bk, "b_v": L0_attn_bv,
        "b_o": L0_attn_bo, "b_xq": L0_xattn_bq, "b_xk": L0_xattn_bk, "b_xv": L0_xattn_bv,
        "b_xo": L0_xattn_bo, "b_ffn": L0_ffn_bias, "alibi": alibi_rows(),
    }
    nc = bacc.Bacc("TRN2", target_bir_lowering=False, num_devices=1)
    arrays, aps = {}, {}
    for name, value in given.items():
        a = np.ascontiguousarray(value)
        arrays[f"in_{name}"] = a
        aps[name] = nc.dram_tensor(f"in_{name}", a.shape, mybir.dt.from_np(a.dtype),
                                   kind="ExternalInput").ap()
    out = nc.dram_tensor("out_y", (NSEQ, T, D), F32, kind="ExternalOutput").ap()
    build(nc, aps["x"], aps["ctx"], {n[2:]: v for n, v in aps.items() if n.startswith("w_")},
          {n[2:]: v for n, v in aps.items() if n.startswith("b_")}, aps["alibi"], out)
    r = run_bass_kernel_spmd(nc, [arrays], core_ids=[0])
    return r.results[0]["out_y"]
```
